# Optimizing a Trainium2 kernel written in Bass

```python
import numpy as np
import jax
import jax.numpy as jnp

def _softmax(x, axis=-1):
    return jax.nn.softmax(x, axis=axis)

def _gelu(x):
    return jax.nn.gelu(x, approximate=True)

def _silu(x):
    return jax.nn.silu(x)

def _sigmoid(x):
    return jax.nn.sigmoid(x)

def _layernorm(x, axis=-1, eps=1e-05):
    m = jnp.mean(x, axis=axis, keepdims=True)
    v = jnp.var(x, axis=axis, keepdims=True)
    return (x - m) / jnp.sqrt(v + eps)

def _scatter_add(tgt, idx, src, axis=0):
    return tgt.at[idx].add(src)

def _segment_sum(src, seg, n):
    return jax.ops.segment_sum(src, seg, n)
kernel_name = 'mk_seq_preln_d1_jaxref_r8_078685'

def setup_inputs(seed: int=0):
    np.random.seed(seed)
    _w = jnp.asarray

    def _L0_attn_setup():
        import jax, jax.numpy as jnp
        import numpy as np
        E = 128
        H = 16
        D = E // H
        WIN = 32
        STRIDE = 128
        G = 1
        B = 2
        L = 4097
        key = jax.random.key(seed)
        ks = jax.random.split(key, 9)
        s = 0.02
        return {'hidden_states': jax.random.normal(ks[0], (B, L, E), jnp.float32), 'Wq': jax.random.normal(ks[1], (E, E), jnp.float32) * s, 'bq': jnp.zeros((E,), jnp.float32), 'Wk': jax.random.normal(ks[2], (E, E), jnp.float32) * s, 'bk': jnp.zeros((E,), jnp.float32), 'Wv': jax.random.normal(ks[3], (E, E), jnp.float32) * s, 'bv': jnp.zeros((E,), jnp.float32), 'Wo': jax.random.normal(ks[4], (E, E), jnp.float32) * s, 'bo': jnp.zeros((E,), jnp.float32)}
    _L0_attn_in = _L0_attn_setup()

    def _L0_ffn_setup():
        import jax, jax.numpy as jnp
        import numpy as np
        NUM_EXPERTS = 8
        TOP_K = 2
        key = jax.random.key(seed)
        ks = jax.random.split(key, 5)
        B, L, E, H, N = (2, 256, 128, 256, NUM_EXPERTS)
        return {'x': jax.random.normal(ks[0], (B, L, E), dtype=jnp.float32), 'gate_kernel': jax.random.normal(ks[1], (E, N), dtype=jnp.float32) / np.sqrt(E), 'w0_kernel': jax.random.normal(ks[2], (N, E, H), dtype=jnp.float32) / np.sqrt(E), 'w1_kernel': jax.random.normal(ks[3], (N, E, H), dtype=jnp.float32) / np.sqrt(E), 'wo_kernel': jax.random.normal(ks[4], (N, H, E), dtype=jnp.float32) / np.sqrt(H)}
    _L0_ffn_in = _L0_ffn_setup()
    _d = {'L0_attn_hidden_states': _L0_attn_in['hidden_states'], 'L0_attn_Wq': _L0_attn_in['Wq'], 'L0_attn_bq': _L0_attn_in['bq'], 'L0_attn_Wk': _L0_attn_in['Wk'], 'L0_attn_bk': _L0_attn_in['bk'], 'L0_attn_Wv': _L0_attn_in['Wv'], 'L0_attn_bv': _L0_attn_in['bv'], 'L0_attn_Wo': _L0_attn_in['Wo'], 'L0_attn_bo': _L0_attn_in['bo'], 'L0_ffn_gate_kernel': _L0_ffn_in['gate_kernel'], 'L0_ffn_w0_kernel': _L0_ffn_in['w0_kernel'], 'L0_ffn_w1_kernel': _L0_ffn_in['w1_kernel'], 'L0_ffn_wo_kernel': _L0_ffn_in['wo_kernel']}
    _x0 = _d['L0_attn_hidden_states']
    _d['L0_attn_hidden_states'] = jax.random.normal(jax.random.fold_in(jax.random.key(seed), 1), (32, 256, 128), dtype=_x0.dtype)
    del _x0
    return _d

def reference(L0_attn_hidden_states, L0_attn_Wq, L0_attn_bq, L0_attn_Wk, L0_attn_bk, L0_attn_Wv, L0_attn_bv, L0_attn_Wo, L0_attn_bo, L0_ffn_gate_kernel, L0_ffn_w0_kernel, L0_ffn_w1_kernel, L0_ffn_wo_kernel):

    def _L0_attn_ref(hidden_states, Wq, bq, Wk, bk, Wv, bv, Wo, bo):
        import jax, jax.numpy as jnp
        import numpy as np
        E = 128
        H = 16
        D = E // H
        WIN = 32
        STRIDE = 128
        G = 1
        B = 2
        L = 4097
        b, seq_len, e = hidden_states.shape
        scale = 1.0 / jnp.sqrt(jnp.asarray(D, hidden_states.dtype))
        q = (hidden_states @ Wq + bq).reshape(b, seq_len, H, D)
        k = (hidden_states @ Wk + bk).reshape(b, seq_len, H, D)
        v = (hidden_states @ Wv + bv).reshape(b, seq_len, H, D)
        qg = q[:, :G]
        gw = jnp.einsum('bghd,bshd->bhgs', qg, k) * scale
        gp = jax.nn.softmax(gw, axis=-1)
        gctx = jnp.einsum('bhgs,bshd->bghd', gp, v).reshape(b, G, e)
        ql, kl, vl = (q[:, G:], k[:, G:], v[:, G:])
        Lc = seq_len - G
        num_windows = max(1, (Lc - WIN) // STRIDE + 1)
        starts = jnp.arange(num_windows) * STRIDE
        widx = starts[:, None] + jnp.arange(WIN)
        qw = ql[:, widx]
        kw = kl[:, widx]
        vw = vl[:, widx]
        aw = jnp.einsum('bwqhd,bwkhd->bwhqk', qw, kw) * scale
        ap = jax.nn.softmax(aw, axis=-1)
        ctx = jnp.einsum('bwhqk,bwkhd->bwqhd', ap, vw)
        ctx = ctx.reshape(b, num_windows * WIN, e)
        flat = widx.reshape(-1)
        local = jnp.zeros((b, Lc, e), hidden_states.dtype).at[:, flat].add(ctx)
        counts = jnp.zeros((Lc,), hidden_states.dtype).at[flat].add(1.0)
        counts = jnp.maximum(counts, 1.0)
        local = local / counts[None, :, None]
        out = jnp.concatenate([gctx, local], axis=1)
        return out @ Wo + bo

    def _L0_ffn_ref(x, gate_kernel, w0_kernel, w1_kernel, wo_kernel):
        import jax, jax.numpy as jnp
        import numpy as np
        NUM_EXPERTS = 8
        TOP_K = 2
        B, L, E = x.shape
        gate_logits = jnp.einsum('ble,en->bln', x, gate_kernel)
        top_k_weights, top_k_indices = jax.lax.top_k(gate_logits, TOP_K)
        softmax_probs = jax.nn.softmax(top_k_weights.astype(jnp.float32), axis=-1)
        weights = jnp.zeros_like(gate_logits)
        b_idx = jnp.arange(B)[:, None, None]
        l_idx = jnp.arange(L)[:, None]
        weights = weights.at[b_idx, l_idx, top_k_indices].set(softmax_probs)
        layer_w0 = jnp.einsum('ble,neh->blnh', x, w0_kernel)
        layer_w1 = jnp.einsum('ble,neh->blnh', x, w1_kernel)
        layer_mult = jax.nn.silu(layer_w0) * layer_w1
        intermediate = jnp.einsum('blnh,nhe->blne', layer_mult, wo_kernel)
        output = jnp.einsum('blne,bln->ble', intermediate, weights)
        return output
    x = L0_attn_hidden_states
    x = x + _L0_attn_ref(_layernorm(x, axis=-1), L0_attn_Wq, L0_attn_bq, L0_attn_Wk, L0_attn_bk, L0_attn_Wv, L0_attn_bv, L0_attn_Wo, L0_attn_bo)
    x = x + _L0_ffn_ref(_layernorm(x, axis=-1), L0_ffn_gate_kernel, L0_ffn_w0_kernel, L0_ffn_w1_kernel, L0_ffn_wo_kernel)
    return x

_drawn_inputs = setup_inputs


def setup_inputs(seed=0):
    import zlib

    import numpy as np

    out = dict(_drawn_inputs(seed))
    spreads = {'L0_attn_bq': (0.0, 0.8),
     'L0_attn_bk': (0.0, 0.8),
     'L0_attn_bv': (0.0, 0.317),
     'L0_attn_bo': (0.0, 0.1)}
    factors = {'L0_attn_Wq': 8.0, 'L0_attn_Wk': 8.0, 'L0_attn_Wv': 3.586}
    for name, (base, spread) in spreads.items():
        noise = np.random.default_rng([zlib.crc32(name.encode()), seed]).standard_normal(out[name].shape)
        drawn = base * np.exp(spread * noise) if base else spread * noise
        out[name] = jnp.asarray(drawn.astype(out[name].dtype))
    for name, factor in factors.items():
        out[name] = (out[name] * factor).astype(out[name].dtype)
    return out
```

```python
import concourse.bass as bass
from concourse import mybir
from contextlib import ExitStack


def preln_attention_moe_kernel(
    nc: bass.Bass,
    x: bass.AP,
    wq: bass.AP,
    bq: bass.AP,
    wk: bass.AP,
    bk: bass.AP,
    wv: bass.AP,
    bv: bass.AP,
    wo: bass.AP,
    bo: bass.AP,
    gate: bass.AP,
    w0: bass.AP,
    w1: bass.AP,
    w2: bass.AP,
    out: bass.AP,
):
    fp32 = mybir.dt.float32
    fp32r = mybir.dt.float32r
    u32 = mybir.dt.uint32
    ALU = mybir.AluOpType
    ACT = mybir.ActivationFunctionType
    AX = mybir.AxisListType

    NSEQ, SEQ, E = x.shape
    NE, _, H = w0.shape
    HEADS, D, WIN = 16, 8, 32
    SCALE = float(D) ** -0.5
    EPS = 1e-5
    P = 128
    NB = 4
    TOK = NB * P
    NT = NSEQ * SEQ // TOK
    NS = TOK // SEQ
    HC = H // P
    K = NE * HC
    LEAD = 3
    HG = HEADS // 4
    QC = WIN + 1
    GR = 32
    NH = 4

    x_v = x.rearrange("s l e -> (s l) e").rearrange("(t j p) e -> t p j e", j=NB, p=P)
    out_v = out.rearrange("s l e -> (s l) e").rearrange("(t j p) e -> t p j e", j=NB, p=P)
    w_rows = nc.dram_tensor("routing_rows", (NT, NE * TOK), fp32).ap()

    ctx = ExitStack()
    with ctx:
        def sb(name, shape, dt=fp32):
            return ctx.enter_context(nc.sbuf_tensor(name, shape, dt))

        def pb(name, shape, dt=fp32):
            return ctx.enter_context(nc.psum_tensor(name, shape, dt))

        def sem(name):
            return ctx.enter_context(nc.semaphore(name))

        ident = sb("ident", [P, P])
        head_mask = sb("head_mask", [P, GR])
        group_mask = sb("group_mask", [P, 4 * D])
        expert_no = sb("expert_no", [P, NE])
        half_power = sb("half_power", [P, NB])
        eps = sb("eps", [P, NB])
        idle = sb("idle", [P, 2])
        Wq, Wk, Wv, Wo, WkT = (sb(n, [P, E]) for n in ("Wq", "Wk", "Wv", "Wo", "WkT"))
        Bq, Bk, Bv = (sb(n, [P, 1]) for n in ("Bq", "Bk", "Bv"))
        Bo = sb("Bo", [P, E])
        G_in = sb("G_in", [P, NE])
        G_hi, G_lo = sb("G_hi", [P, NE], fp32r), sb("G_lo", [P, NE], fp32r)
        W2_in = sb("W2_in", [P, NE * H])
        W_hi, W_lo = sb("W_hi", [P, 3, NE * H], fp32r), sb("W_lo", [P, 3, NE * H], fp32r)

        X = sb("X", [P, NT * TOK])

        stats1, stats2 = sb("stats1", [P, NB, 6]), sb("stats2", [P, NB, 6])
        mv1, mv2 = sb("mv1", [P, NB, 2]), sb("mv2", [P, NB, 2])
        var1, var2 = sb("var1", [P, NB]), sb("var2", [P, NB])
        rstd1, rstd2 = sb("rstd1", [P, NB]), sb("rstd2", [P, NB])
        mr1, mr2 = sb("mr1", [P, NB]), sb("mr2", [P, NB])
        shift1, shift2 = sb("shift1", [P, NB]), sb("shift2", [P, NB])
        xn1, xn2 = sb("xn1", [P, NB, E]), sb("xn2", [P, NB, E])
        xT = sb("xT", [P, TOK])
        xT_win = sb("xT_win", [P, NB, 4, WIN])
        QT, KT = sb("QT", [P, NB, QC]), sb("KT", [P, NB, WIN])
        q_glob = sb("q_glob", [P, NS, GR])
        q_heads = sb("q_heads", [P, NB, HEADS, WIN])
        v_heads = sb("v_heads", [P, NB, E])
        U, c_glob = sb("U", [P, NS * GR]), sb("c_glob", [NS * GR, 1])
        sg, pg = sb("sg", [NS * GR, SEQ]), sb("pg", [NS * GR, SEQ])
        pgn = sb("pgn", [NS * GR, SEQ])
        gmax, gshift, gsum, grec = (sb(n, [NS * GR, 1]) for n in ("gmax", "gshift", "gsum", "grec"))
        pgT = sb("pgT", [P, 2, NS * GR])
        gmix = sb("gmix", [P, NS * GR])
        zmask, zctx = sb("zmask", [P, NS, GR]), sb("zctx", [P, NS])
        wmax, wsum, wrec = (sb(n, [P, HG * NB]) for n in ("wmax", "wsum", "wrec"))
        ws, wp, wpn, wpT = (sb(n, [P, TOK]) for n in ("ws", "wp", "wpn", "wpT"))
        C = sb("C", [P, NB, QC])

        lg, top = sb("lg", [P, NB, NE]), sb("top", [P, NB, 8])
        top_no, top_nof = sb("top_no", [P, NB, 8], u32), sb("top_nof", [P, NB, 2])
        gap, tanh_gap = sb("gap", [P, NB]), sb("tanh_gap", [P, NB])
        share = sb("share", [P, 2, NB])
        pick = sb("pick", [P, 2, NE, NB])
        picked = sb("picked", [P, 2, NE, NB])
        W_tok = sb("W_tok", [P, NE, NB])
        w_tile = sb("w_tile", [NE * NB, P])

        Wb = sb("Wb", [P, 2, NE * TOK])
        W_in = [Wb[:, 1, 0:NE * H], Wb[:, 1, NE * H:2 * NE * H], W2_in[:]]
        x_hi, x_lo = sb("x_hi", [P, 2, TOK], fp32r), sb("x_lo", [P, 2, TOK], fp32r)
        sil, silw, hid = sb("sil", [P, 2, TOK]), sb("silw", [P, 2, TOK]), sb("hid", [P, 2, TOK])
        h_hi, h_lo = sb("h_hi", [P, NH, TOK], fp32r), sb("h_lo", [P, NH, TOK], fp32r)
        yT = sb("yT", [P, TOK])
        y_out = sb("y_out", [P, 2, NB, E])

        AB = pb("AB", [P, 2, 2, TOK])
        YB = pb("YB", [P, TOK])
        P0, P1, P2 = pb("P0", [P, TOK]), pb("P1", [P, TOK]), pb("P2", [P, TOK])

        x_in = [sem("x_in0"), sem("x_in1")]
        small_in, moe_in = sem("small_in"), sem("moe_in")
        consts_ready, ident_ready, wkT_done, wkT_ready = (
            sem(n) for n in ("consts_ready", "ident_ready", "wkT_done", "wkT_ready"))
        w_hi_ready, w_lo_ready = sem("w_hi_ready"), sem("w_lo_ready")
        (stats1_ready, scale1_ready, xn1_ready, T1_done, xT_ready, QK_done, QT_ready, KT_ready,
         q_glob_ready, q_heads_ready, U_done, U_ready, V_done, v_heads_ready, G_done, sg_ready,
         pg_ready, pgn_ready, S_done, ws_ready, wp_ready, wrec_ready, wpn_ready, wpT_ready,
         pgT_done, pgT_ready, mix_done, gmix_ready, Z_done, zctx_ready, CT_done, C_ready,
         O_done, bo_added, x1_ready, stats2_ready, scale2_ready, xn2_ready, T2_done, x_hi_ready,
         x_lo_ready, logits_done, lg_ready, gap_ready, tanh_ready, share_ready, W_tok_ready,
         WT_done, w_tile_ready) = (
            sem(n) for n in (
                "stats1_ready", "scale1_ready", "xn1_ready", "T1_done", "xT_ready", "QK_done",
                "QT_ready", "KT_ready", "q_glob_ready", "q_heads_ready", "U_done", "U_ready",
                "V_done", "v_heads_ready", "G_done", "sg_ready", "pg_ready", "pgn_ready",
                "S_done", "ws_ready", "wp_ready", "wrec_ready", "wpn_ready", "wpT_ready",
                "pgT_done", "pgT_ready", "mix_done", "gmix_ready", "Z_done", "zctx_ready",
                "CT_done", "C_ready", "O_done", "bo_added", "x1_ready", "stats2_ready",
                "scale2_ready", "xn2_ready", "T2_done", "x_hi_ready", "x_lo_ready",
                "logits_done", "lg_ready", "gap_ready", "tanh_ready", "share_ready",
                "W_tok_ready", "WT_done", "w_tile_ready"))
        rows_out = sem("rows_out")
        wb_in = [sem("wb_in0"), sem("wb_in1")]
        A_done, B_done, sil_ready, silw_ready, hid_ready, h_hi_ready, h_lo_ready, Y_done = (
            sem(n) for n in ("A_done", "B_done", "sil_ready", "silw_ready", "hid_ready",
                             "h_hi_ready", "h_lo_ready", "Y_done"))
        yT_ready, OT_done, y_ready = sem("yT_ready"), sem("OT_done"), sem("y_ready")
        stored = [sem("stored0"), sem("stored1")]

        def need(eng, s, n):
            if not (isinstance(n, int) and n <= 0):
                eng.wait_ge(s, n)

        def tile_of(X_, a, rows=P):
            return X_[0:rows, bass.ds(a * TOK, TOK)]

        def over_tiles(eng, macro):
            macro(0, 0, True, True)
            with eng.Fori(0, (NT - 4) // 2, 1) as i:
                macro(i * 2 + 1, 1, True, True)
                macro(i * 2 + 2, 0, True, True)
            macro(NT - 3, (NT - 3) % 2, True, True)
            macro(NT - 2, (NT - 2) % 2, True, False)
            macro(NT - 1, (NT - 1) % 2, False, False)

        block = ctx.enter_context(nc.Block())

        @block.sync
        def _(sp):
            def load_x(a, u):
                need(sp, x_in[u], (a - u) // 2 * 16 if isinstance(a, int) else (a - u) * 8)
                sp.dma_start(tile_of(X, a).rearrange("p (j e) -> p j e", j=NB),
                             x_v[bass.ds(a, 1)].rearrange("a p j e -> (a p) j e")
                             if not isinstance(a, int) else x_v[a]).then_inc(x_in[u], 16)

            load_x(0, 0)
            for dst, src in ((Wq, wq), (Wk, wk), (Wv, wv), (Wo, wo), (G_in, gate)):
                sp.dma_start(dst[:], src).then_inc(small_in, 16)
            for dst, src in ((Bq, bq), (Bk, bk), (Bv, bv)):
                sp.dma_start(dst[:], src.rearrange("(p o) -> p o", o=1)).then_inc(small_in, 16)
            sp.dma_start(Bo[:], bo.rearrange("(o e) -> o e", o=1).broadcast_to([P, E])).then_inc(small_in, 16)
            load_x(1, 1)
            with sp.Fori(1, NT // 2, 1) as i:
                load_x(i * 2, 0)
                load_x(i * 2 + 1, 1)

            def spread_routing(a, u):
                if isinstance(a, int) and a == 1:
                    sp.wait_ge(w_lo_ready, 4)
                sp.wait_ge(w_tile_ready, a + 1)
                sp.dma_start(w_rows[bass.ds(a, 1)].rearrange("o (r p) -> (o r) p", p=P), w_tile[:]).then_inc(rows_out, 16)
                sp.wait_ge(rows_out, a * 16 + 16)
                half = NE * TOK // 2
                for q in range(2):
                    sp.dma_start(Wb[:, u, q * half:(q + 1) * half],
                                 w_rows[bass.ds(a, 1), q * half:(q + 1) * half].broadcast_to([P, half])).then_inc(wb_in[q], 16)

            def store(t, u):
                sp.wait_ge(y_ready, t + 1)
                dst = out_v[t] if isinstance(t, int) else out_v[bass.ds(t, 1)].rearrange("a p j e -> (a p) j e")
                sp.dma_start(dst, y_out[:, u]).then_inc(stored[u], 16)

            def macro(t, u, second, first):
                if not (isinstance(t, int) and t == 0):
                    store(t - 1, 1 - u)
                if second:
                    spread_routing(t + 1, 1 - u)

            spread_routing(0, 0)
            over_tiles(sp, macro)
            store(NT - 1, (NT - 1) % 2)
            for u in range(2):
                sp.wait_ge(stored[u], NT // 2 * 16)

        @block.gpsimd
        def _(pool):
            g = nc.gpsimd
            g.memset(ident[:], 0.0)
            g.memset(head_mask[:], 1.0)
            g.memset(group_mask[:], 1.0)
            g.memset(half_power[:], -0.5)
            g.memset(eps[:], EPS)
            g.memset(C[:], 0.0)
            for n in range(NE):
                g.memset(expert_no[:, n:n + 1], float(n))
            pool.drain()
            g.affine_select(out=ident[:], in_=ident[:], compare_op=ALU.not_equal, fill=1.0, base=0,
                            pattern=[[-1, P]], channel_multiplier=1).then_inc(ident_ready, 1)
            g.affine_select(out=head_mask[:], in_=head_mask[:], compare_op=ALU.is_ge, fill=0.0, base=0,
                            pattern=[[-D, GR]], channel_multiplier=1)
            gm = group_mask[:].rearrange("p (g d) -> p g d", d=D)
            g.affine_select(out=gm, in_=gm, compare_op=ALU.is_ge, fill=0.0, base=0,
                            pattern=[[-WIN, 4], [0, D]], channel_multiplier=1)
            pool.drain()
            g.affine_select(out=head_mask[:], in_=head_mask[:], compare_op=ALU.is_ge, fill=0.0, base=D - 1,
                            pattern=[[D, GR]], channel_multiplier=-1)
            g.affine_select(out=gm, in_=gm, compare_op=ALU.is_ge, fill=0.0, base=WIN - 1,
                            pattern=[[WIN, 4], [0, D]], channel_multiplier=-1).then_inc(consts_ready, 1)
            pool.drain()

            def norm_scale(a, stats_ready, mv, var, rstd, mr, shift, used, ready):
                pool.wait_ge(stats_ready, a + 1)
                need(pool, used, a)
                g.tensor_tensor(var[:], mv[:, :, 1], eps[:], ALU.add)
                pool.drain()
                g.tensor_tensor(rstd[:], var[:], half_power[:], ALU.pow)
                pool.drain()
                g.tensor_tensor(mr[:], mv[:, :, 0], rstd[:], ALU.mult)
                pool.drain()
                g.tensor_scalar(shift[:], mr[:], -1.0, None, ALU.mult).then_inc(ready, 1)

            def scale1(a):
                norm_scale(a, stats1_ready, mv1, var1, rstd1, mr1, shift1, xn1_ready, scale1_ready)

            def scale2(a):
                norm_scale(a, stats2_ready, mv2, var2, rstd2, mr2, shift2, xn2_ready, scale2_ready)

            def spread_q_glob(a):
                pool.wait_ge(QT_ready, a + 1)
                need(pool, U_done, a)
                g.tensor_tensor(q_glob[:], QT[:, 0:NB:2, 0:1].broadcast_to([P, NS, GR]),
                                head_mask[:].unsqueeze(1).broadcast_to([P, NS, GR]), ALU.mult).then_inc(q_glob_ready, 1)

            def spread_q_heads(a, w):
                if w == 0:
                    need(pool, S_done, a)
                ins = g.tensor_tensor(q_heads[:, w], QT[:, w, 1:QC].unsqueeze(1).broadcast_to([P, HEADS, WIN]),
                                      head_mask[:, 0:HEADS].unsqueeze(2).broadcast_to([P, HEADS, WIN]), ALU.mult)
                if w == NB - 1:
                    ins.then_inc(q_heads_ready, 1)

            def add_bo(a):
                pool.wait_ge(xn1_ready, a + 1)
                xt = tile_of(X, a).rearrange("p (j e) -> p j e", j=NB)
                g.tensor_tensor(xt, xt, Bo[:].unsqueeze(1).broadcast_to([P, NB, E]), ALU.add).then_inc(bo_added, 1)

            def window_probs(a):
                pool.wait_ge(wrec_ready, a + 1)
                need(pool, wpT_ready, a)
                g.tensor_tensor(wpn[:].rearrange("p (b k) -> p b k", k=WIN), wp[:].rearrange("p (b k) -> p b k", k=WIN),
                                wrec[:].unsqueeze(2).broadcast_to([P, HG * NB, WIN]), ALU.mult).then_inc(wpn_ready, 1)

            def token_weights(a):
                pool.wait_ge(share_ready, a + 1)
                need(pool, WT_done, a)
                g.tensor_tensor(picked[:], pick[:], share[:].unsqueeze(2).broadcast_to([P, 2, NE, NB]), ALU.mult)
                pool.drain()
                g.tensor_tensor(W_tok[:], picked[:, 0], picked[:, 1], ALU.add).then_inc(W_tok_ready, 1)

            def weight(t, u, k):
                if k == 0:
                    pool.wait_ge(wb_in[0], t * 16 + 16)
                if k == K // 2:
                    pool.wait_ge(wb_in[1], t * 16 + 16)
                pool.wait_ge(sil_ready, t * K + k + 1)
                need(pool, hid_ready, t * K + k - 1)
                n = k // HC
                g.tensor_tensor(silw[:, k % 2], sil[:, k % 2], Wb[:, u, n * TOK:(n + 1) * TOK], ALU.mult).then_inc(silw_ready, 1)

            def first_half(a):
                scale1(a)
                spread_q_glob(a)
                for w in range(NB):
                    spread_q_heads(a, w)
                window_probs(a)

            def macro(t, u, second, first):
                for k in range(K):
                    weight(t, u, k)
                    if second and k == 1:
                        add_bo(t + 1)
                    if first and k == 3:
                        scale1(t + 2)
                    if second and k == 7:
                        scale2(t + 1)
                    if first and k == 8:
                        spread_q_glob(t + 2)
                    if first and 8 <= k < 12:
                        spread_q_heads(t + 2, k - 8)
                    if second and k == 11:
                        token_weights(t + 1)
                    if first and k == 15:
                        window_probs(t + 2)

            pool.wait_ge(small_in, 9 * 16)
            first_half(0)
            add_bo(0)
            scale2(0)
            token_weights(0)
            first_half(1)
            over_tiles(pool, macro)

        @block.scalar
        def _(act):
            s = nc.scalar

            def normalise(a, j, xn, scale_ready, rstd, shift, used, ready):
                if j == 0:
                    act.wait_ge(scale_ready, a + 1)
                    need(act, used, a)
                    s.activation(idle[:, 0:1], rstd[:, 0:1], ACT.Copy)
                ins = s.activation(xn[:, j], X[:, bass.ds(a * TOK + j * E, E)], ACT.Identity,
                                   scale=rstd[:, j:j + 1], bias=shift[:, j:j + 1])
                if j == NB - 1:
                    ins.then_inc(ready, 1)

            def normalise1(a, j):
                normalise(a, j, xn1, scale1_ready, rstd1, shift1, mix_done, xn1_ready)

            def normalise2(a, j):
                normalise(a, j, xn2, scale2_ready, rstd2, shift2, T2_done, xn2_ready)

            def keep_xT(a):
                act.wait_ge(T1_done, a + 1)
                need(act, G_done, a)
                s.activation(xT[:], P0[:], ACT.Identity)
                win = P0[:].rearrange("p (j q) -> p j q", q=P)[:, :, 1:QC]
                s.activation(xT_win[:], win.unsqueeze(2).broadcast_to([P, NB, 4, WIN]), ACT.Identity).then_inc(xT_ready, 1)

            def keep_qk(a):
                act.wait_ge(QK_done, a + 1)
                need(act, q_heads_ready, a)
                need(act, S_done, a)
                nq = NB * QC
                s.activation(QT[:], P0[:, 0:nq].rearrange("p (j q) -> p j q", q=QC), ACT.Identity,
                             bias=Bq[:, 0:1]).then_inc(QT_ready, 1)
                s.activation(KT[:], P0[:, nq:nq + NB * WIN].rearrange("p (j q) -> p j q", q=WIN), ACT.Identity,
                             bias=Bk[:, 0:1]).then_inc(KT_ready, 1)

            def keep_U(a):
                act.wait_ge(U_done, a + 1)
                need(act, sg_ready, a)
                s.activation(c_glob[:], P0[0:NS * GR, NS * GR:NS * GR + 1], ACT.Identity)
                s.activation(U[:], P0[:, 0:NS * GR], ACT.Identity).then_inc(U_ready, 1)

            def exps(a):
                act.wait_ge(sg_ready, a + 1)
                need(act, pgn_ready, a)
                s.activation(pg[:], sg[:], ACT.Exp, scale=SCALE, bias=gshift[:, 0:1],
                             accum_out=gsum[:, 0:1]).then_inc(pg_ready, 1)
                act.wait_ge(ws_ready, a + 1)
                need(act, wpn_ready, a)
                s.activation(wp[:], ws[:], ACT.Exp, scale=SCALE).then_inc(wp_ready, 1)

            def keep_context(a):
                act.wait_ge(CT_done, a + 1)
                need(act, O_done, a)
                s.activation(C[:, :, 1:QC], P1[:, 0:NB * WIN].rearrange("p (j q) -> p j q", q=WIN), ACT.Identity,
                             bias=Bv[:, 0:1]).then_inc(C_ready, 1)

            def split_x(a, u):
                act.wait_ge(T2_done, a + 1)
                need(act, B_done, a * K - K)
                s.activation(x_hi[:, u], P0[:], ACT.Copy).then_inc(x_hi_ready, 1)

            def keep_logits(a):
                act.wait_ge(logits_done, a + 1)
                need(act, share_ready, a)
                s.activation(lg[:], P0[:, 0:NB * NE].rearrange("p (j n) -> p j n", n=NE), ACT.Copy).then_inc(lg_ready, 1)

            def tanh(a):
                act.wait_ge(gap_ready, a + 1)
                s.activation(tanh_gap[:], gap[:], ACT.Tanh, scale=0.5).then_inc(tanh_ready, 1)

            def keep_w_tile(a):
                act.wait_ge(WT_done, a + 1)
                need(act, rows_out, a * 16)
                s.activation(w_tile[:], P0[0:NE * NB, 0:P], ACT.Copy).then_inc(w_tile_ready, 1)

            def silu(t, k):
                act.wait_ge(A_done, t * K + k + 1)
                need(act, silw_ready, t * K + k - 1)
                s.activation(sil[:, k % 2], AB[:, k % 2, 0], ACT.Silu).then_inc(sil_ready, 1)

            def split_h(t, k):
                act.wait_ge(hid_ready, t * K + k + 1)
                need(act, Y_done, t * K + k - NH + 1)
                s.activation(h_hi[:, k % NH], hid[:, k % 2], ACT.Copy).then_inc(h_hi_ready, 1)

            def keep_y(t):
                act.wait_ge(Y_done, t * K + K)
                need(act, OT_done, t)
                s.activation(yT[:], YB[:], ACT.Copy).then_inc(yT_ready, 1)

            def first_half(a):
                for j in range(NB):
                    normalise1(a, j)
                keep_xT(a)
                keep_qk(a)
                keep_U(a)
                exps(a)

            def macro(t, u, second, first):
                zero = isinstance(t, int) and t == 0
                for k in range(K):
                    silu(t, k)
                    if k > 0:
                        split_h(t, k - 1)
                    elif not zero:
                        split_h(t - 1, K - 1)
                    if k == 2 and not zero:
                        keep_y(t - 1)
                    if second and k == 3:
                        keep_context(t + 1)
                    if first and k in (4, 5):
                        for j in (2 * k - 8, 2 * k - 7):
                            normalise1(t + 2, j)
                    if first and k == 6:
                        keep_xT(t + 2)
                    if first and k == 7:
                        keep_qk(t + 2)
                    if first and k == 8:
                        keep_U(t + 2)
                    if second and k == 8:
                        for j in range(NB):
                            normalise2(t + 1, j)
                    if second and k == 9:
                        split_x(t + 1, 1 - u)
                    if second and k == 10:
                        keep_logits(t + 1)
                    if second and k == 11:
                        tanh(t + 1)
                    if second and k == 12:
                        keep_w_tile(t + 1)
                    if first and k == 13:
                        exps(t + 2)

            act.dma_start(W_in[0].rearrange("p (n h) -> p n h", n=NE), w0.rearrange("n e h -> e n h")).then_inc(moe_in, 16)
            act.dma_start(W_in[1].rearrange("p (n h) -> p n h", n=NE), w1.rearrange("n e h -> e n h")).then_inc(moe_in, 16)
            act.dma_start(W_in[2].rearrange("p (n e) -> p n e", e=E), w2.rearrange("n (c p) e -> p (n c) e", p=P)).then_inc(moe_in, 16)
            act.wait_ge(small_in, 9 * 16)
            act.wait_ge(consts_ready, 1)
            act.wait_ge(wkT_done, 1)
            s.activation(WkT[:], P0[:, 0:P], ACT.Identity).then_inc(wkT_ready, 1)
            s.activation(G_hi[:], G_in[:], ACT.Copy).then_inc(w_hi_ready, 1)
            first_half(0)
            act.wait_ge(moe_in, 3 * 16)
            for m in range(3):
                s.activation(W_hi[:, m], W_in[m], ACT.Copy).then_inc(w_hi_ready, 1)
            keep_context(0)
            for j in range(NB):
                normalise2(0, j)
            split_x(0, 0)
            keep_logits(0)
            tanh(0)
            keep_w_tile(0)
            first_half(1)
            over_tiles(act, macro)
            split_h(NT - 1, K - 1)
            keep_y(NT - 1)

        @block.vector
        def _(dve):
            v = nc.vector

            def statistics(a, stats, mv, used, ready):
                need(dve, used, a)
                v.memset(idle[:, 1:2], 0.0)
                for j in range(NB):
                    v.bn_stats(stats[:, j], X[:, bass.ds(a * TOK + j * E, E)])
                dve.drain()
                for j in range(NB):
                    last = v.bn_aggr(mv[:, j], stats[:, j])
                last.then_inc(ready, 1)

            def statistics1(a, u):
                dve.wait_ge(x_in[u], (a - u) // 2 * 16 + 16 if isinstance(a, int) else (a - u) * 8 + 16)
                statistics(a, stats1, mv1, scale1_ready, stats1_ready)

            def statistics2(a):
                dve.wait_ge(x1_ready, a + 1)
                statistics(a, stats2, mv2, scale2_ready, stats2_ready)

            def spread_v(a):
                dve.wait_ge(V_done, a + 1)
                need(dve, CT_done, a)
                v.tensor_tensor(v_heads[:].rearrange("p w (c m) -> p (w c) m", m=4 * D),
                                P1[:].rearrange("p (b m) -> p b m", m=4 * D),
                                group_mask[:].unsqueeze(1).broadcast_to([P, HG * NB, 4 * D]), ALU.mult).then_inc(v_heads_ready, 1)

            def global_scores(a):
                dve.wait_ge(G_done, a + 1)
                dve.wait_ge(U_ready, a + 1)
                need(dve, pg_ready, a)
                v.tensor_scalar(sg[:], P2[0:NS * GR, 0:SEQ], c_glob[:, 0:1], None, ALU.add)
                dve.drain()
                v.tensor_reduce(gmax[:], sg[:], AX.X, ALU.max)
                dve.drain()
                v.tensor_scalar(gshift[:], gmax[:], -SCALE, None, ALU.mult).then_inc(sg_ready, 1)

            def window_scores(a):
                dve.wait_ge(S_done, a + 1)
                need(dve, wp_ready, a)
                sc = P1[:].rearrange("p (b k) -> p b k", k=WIN)
                v.tensor_reduce(wmax[:], sc, AX.X, ALU.max)
                dve.drain()
                v.tensor_tensor(ws[:].rearrange("p (b k) -> p b k", k=WIN), sc,
                                wmax[:].unsqueeze(2).broadcast_to([P, HG * NB, WIN]), ALU.subtract).then_inc(ws_ready, 1)

            def global_probs(a):
                dve.wait_ge(pg_ready, a + 1)
                need(dve, pgT_done, a)
                v.reciprocal(grec[:], gsum[:])
                dve.drain()
                v.tensor_scalar(pgn[:], pg[:], grec[:, 0:1], None, ALU.mult).then_inc(pgn_ready, 1)

            def window_sums(a):
                dve.wait_ge(wp_ready, a + 1)
                need(dve, wpn_ready, a)
                v.tensor_reduce(wsum[:], wp[:].rearrange("p (b k) -> p b k", k=WIN), AX.X, ALU.add)
                dve.drain()
                v.reciprocal(wrec[:], wsum[:]).then_inc(wrec_ready, 1)

            def turn_probs(a):
                dve.wait_ge(wpn_ready, a + 1)
                need(dve, CT_done, a)
                v.transpose(wpT[:], wpn[:]).then_inc(wpT_ready, 1)

            def keep_pgT(a):
                dve.wait_ge(pgT_done, a + 1)
                need(dve, mix_done, a)
                v.tensor_copy(pgT[:], P2[:, 0:2 * NS * GR].rearrange("p (c r) -> p c r", c=2)).then_inc(pgT_ready, 1)

            def keep_mix(a):
                dve.wait_ge(mix_done, a + 1)
                need(dve, Z_done, a)
                v.tensor_copy(gmix[:], P2[:, 0:NS * GR]).then_inc(gmix_ready, 1)

            def global_context(a):
                dve.wait_ge(Z_done, a + 1)
                need(dve, O_done, a)
                v.tensor_tensor(zmask[:], P2[:, 0:NS * GR].rearrange("p (s h) -> p s h", s=NS),
                                head_mask[:].unsqueeze(1).broadcast_to([P, NS, GR]), ALU.mult)
                dve.drain()
                v.tensor_reduce(zctx[:], zmask[:], AX.X, ALU.add)
                dve.drain()
                v.tensor_scalar(C[:, 0:NB:2, 0], zctx[:], Bv[:, 0:1], None, ALU.add).then_inc(zctx_ready, 1)

            def add_attention(a):
                dve.wait_ge(O_done, a + 1)
                dve.wait_ge(bo_added, a + 1)
                xt = tile_of(X, a, QC)
                v.tensor_tensor(xt, xt, P1[0:QC, :], ALU.add).then_inc(x1_ready, 1)

            def rest_x(a, u):
                dve.wait_ge(x_hi_ready, a + 1)
                need(dve, B_done, a * K - K)
                v.tensor_tensor(x_lo[:, u], P0[:], x_hi[:, u], ALU.subtract).then_inc(x_lo_ready, 1)

            def top_two(a):
                dve.wait_ge(lg_ready, a + 1)
                need(dve, W_tok_ready, a)
                v.memset(idle[:, 1:2], 0.0)
                for j in range(NB):
                    v.max(top[:, j], lg[:, j])
                dve.drain()
                v.tensor_tensor(gap[:], top[:, :, 0], top[:, :, 1], ALU.subtract).then_inc(gap_ready, 1)
                for j in range(NB):
                    v.max_index(top_no[:, j], top[:, j], lg[:, j])
                dve.drain()
                v.tensor_copy(top_nof[:], top_no[:, :, 0:2])
                dve.drain()
                for r in range(2):
                    v.tensor_tensor(pick[:, r], expert_no[:].unsqueeze(2).broadcast_to([P, NE, NB]),
                                    top_nof[:, :, r].unsqueeze(1).broadcast_to([P, NE, NB]), ALU.is_equal)
                dve.wait_ge(tanh_ready, a + 1)
                v.tensor_scalar(share[:, 0], tanh_gap[:], 0.5, 0.5, ALU.mult, ALU.add)
                v.tensor_scalar(share[:, 1], tanh_gap[:], -0.5, 0.5, ALU.mult, ALU.add).then_inc(share_ready, 1)

            def hidden(t, k):
                dve.wait_ge(silw_ready, t * K + k + 1)
                dve.wait_ge(B_done, t * K + k + 1)
                need(dve, h_lo_ready, t * K + k - 1)
                v.tensor_tensor(hid[:, k % 2], silw[:, k % 2], AB[:, k % 2, 1], ALU.mult).then_inc(hid_ready, 1)

            def rest_h(t, k):
                dve.wait_ge(h_hi_ready, t * K + k + 1)
                need(dve, Y_done, t * K + k - NH + 1)
                v.tensor_tensor(h_lo[:, k % NH], hid[:, k % 2], h_hi[:, k % NH], ALU.subtract).then_inc(h_lo_ready, 1)

            def finish(t, u):
                dve.wait_ge(OT_done, t + 1)
                need(dve, stored[u], (t - u) // 2 * 16 if isinstance(t, int) else (t - u) * 8)
                v.tensor_tensor(y_out[:, u].rearrange("p j e -> p (j e)"), P1[:], tile_of(X, t), ALU.add).then_inc(y_ready, 1)

            def first_half(a, u):
                statistics1(a, u)
                spread_v(a)
                global_scores(a)
                window_scores(a)
                global_probs(a)
                window_sums(a)

            def macro(t, u, second, first):
                zero = isinstance(t, int) and t == 0
                for k in range(K):
                    hidden(t, k)
                    if k > 0:
                        rest_h(t, k - 1)
                    elif not zero:
                        rest_h(t - 1, K - 1)
                    if second and k == 0:
                        turn_probs(t + 1)
                    if first and k == 2:
                        statistics1(t + 2, u)
                    if second and k == 3:
                        keep_pgT(t + 1)
                    if second and k == 4:
                        keep_mix(t + 1)
                    if second and k == 5:
                        global_context(t + 1)
                    if second and k == 6:
                        add_attention(t + 1)
                        statistics2(t + 1)
                    if k == 7 and not zero:
                        finish(t - 1, 1 - u)
                    if first and k == 8:
                        spread_v(t + 2)
                    if second and k == 9:
                        rest_x(t + 1, 1 - u)
                    if first and k == 10:
                        global_scores(t + 2)
                    if second and k == 11:
                        top_two(t + 1)
                    if first and k == 12:
                        window_scores(t + 2)
                    if first and k == 14:
                        global_probs(t + 2)
                        window_sums(t + 2)

            dve.wait_ge(consts_ready, 1)
            dve.wait_ge(w_hi_ready, 1)
            v.tensor_tensor(G_lo[:], G_in[:], G_hi[:], ALU.subtract).then_inc(w_lo_ready, 1)
            first_half(0, 0)
            for m in range(3):
                dve.wait_ge(w_hi_ready, m + 2)
                v.tensor_tensor(W_lo[:, m], W_in[m], W_hi[:, m], ALU.subtract).then_inc(w_lo_ready, 1)
            turn_probs(0)
            keep_pgT(0)
            keep_mix(0)
            global_context(0)
            add_attention(0)
            statistics2(0)
            rest_x(0, 0)
            top_two(0)
            first_half(1, 1)
            over_tiles(dve, macro)
            rest_h(NT - 1, K - 1)
            finish(NT - 1, (NT - 1) % 2)

        @block.tensor
        def _(pe):
            mm = nc.tensor.matmul

            def turn_x1(a):
                pe.wait_ge(xn1_ready, a + 1)
                need(pe, U_ready, a)
                need(pe, w_tile_ready, a - 1)
                for j in range(NB):
                    last = nc.tensor.transpose(P0[:, j * P:(j + 1) * P], xn1[:, j], ident[:])
                last.then_inc(T1_done, 1)

            def project_qk(a):
                pe.wait_ge(xT_ready, a + 1)
                xw = xT[:].rearrange("p (j q) -> p j q", q=P)
                nq = NB * QC
                mm(P0[:, 0:nq], Wq[:], xw[:, :, 0:QC], start=True, stop=True)
                mm(P0[:, nq:nq + NB * WIN], Wk[:], xw[:, :, 1:QC], start=True, stop=True).then_inc(QK_done, 1)

            def project_v(a):
                pe.wait_ge(xT_ready, a + 1)
                need(pe, x1_ready, a)
                need(pe, y_ready, a - 2)
                for w in range(NB):
                    last = mm(P1[:, w * E:(w + 1) * E], xT_win[:, w].rearrange("p r k -> p (r k)"), Wv[:], start=True, stop=True)
                last.then_inc(V_done, 1)

            def fold_keys(a):
                pe.wait_ge(q_glob_ready, a + 1)
                pe.wait_ge(KT_ready, a + 1)
                qg = q_glob[:].rearrange("p s h -> p (s h)")
                mm(P0[:, 0:NS * GR], WkT[:], qg, start=True, stop=True)
                mm(P0[0:NS * GR, NS * GR:NS * GR + 1], qg, Bk[:], start=True, stop=True).then_inc(U_done, 1)

            def score_global(a):
                pe.wait_ge(U_ready, a + 1)
                need(pe, zctx_ready, a)
                for b in range(NS):
                    last = mm(P2[b * GR:(b + 1) * GR, 0:SEQ], U[:, b * GR:(b + 1) * GR],
                              xT[:, b * SEQ:(b + 1) * SEQ], start=True, stop=True)
                last.then_inc(G_done, 1)

            def score_windows(a):
                pe.wait_ge(q_heads_ready, a + 1)
                pe.wait_ge(KT_ready, a + 1)
                pe.wait_ge(v_heads_ready, a + 1)
                for c in range(HG):
                    for w in range(NB):
                        col = (c * NB + w) * WIN
                        q = q_heads[:, w, 4 * c:4 * c + 4].rearrange("p h q -> p (h q)")
                        last = mm(P1[:, col:col + WIN], q, KT[:, w], start=True, stop=True)
                last.then_inc(S_done, 1)

            def turn_global_probs(a):
                pe.wait_ge(pgn_ready, a + 1)
                pe.wait_ge(sg_ready, a + 1)
                r = NS * GR
                for c in range(SEQ // P):
                    last = mm(P2[:, c * r:(c + 1) * r], pgn[:, c * P:(c + 1) * P], ident[0:r, 0:r], start=True, stop=True)
                last.then_inc(pgT_done, 1)

            def mix_global(a):
                pe.wait_ge(pgT_ready, a + 1)
                for b in range(NS):
                    for c in range(SEQ // P):
                        last = mm(P2[:, b * GR:(b + 1) * GR], xn1[:, b * 2 + c], pgT[:, c, b * GR:(b + 1) * GR],
                                  start=(c == 0), stop=(c == SEQ // P - 1))
                last.then_inc(mix_done, 1)

            def project_mix(a):
                pe.wait_ge(gmix_ready, a + 1)
                mm(P2[:, 0:NS * GR], Wv[:], gmix[:], start=True, stop=True).then_inc(Z_done, 1)

            def window_context(a):
                pe.wait_ge(wpT_ready, a + 1)
                pe.wait_ge(v_heads_ready, a + 1)
                pe.wait_ge(ws_ready, a + 1)
                for w in range(NB):
                    for c in range(HG):
                        col = (c * NB + w) * WIN
                        last = mm(P1[32 * c:32 * (c + 1), w * WIN:(w + 1) * WIN], v_heads[:, w, 32 * c:32 * (c + 1)],
                                  wpT[:, col:col + WIN], start=True, stop=True)
                last.then_inc(CT_done, 1)

            def project_out(a):
                pe.wait_ge(C_ready, a + 1)
                pe.wait_ge(zctx_ready, a + 1)
                for j in range(NB):
                    last = mm(P1[0:QC, j * E:(j + 1) * E], C[:, j], Wo[:], start=True, stop=True)
                last.then_inc(O_done, 1)

            def turn_x2(a, after):
                pe.wait_ge(xn2_ready, a + 1)
                need(pe, U_ready, after)
                for j in range(NB):
                    last = nc.tensor.transpose(P0[:, j * P:(j + 1) * P], xn2[:, j], ident[:])
                last.then_inc(T2_done, 1)

            def score_experts(a, u):
                pe.wait_ge(x_lo_ready, a + 1)
                for j in range(NB):
                    sl = slice(j * P, (j + 1) * P)
                    dst = P0[:, j * NE:(j + 1) * NE]
                    mm(dst, x_hi[:, u, sl], G_hi[:], start=True, stop=False)
                    mm(dst, x_hi[:, u, sl], G_lo[:], start=False, stop=False)
                    last = mm(dst, x_lo[:, u, sl], G_hi[:], start=False, stop=True)
                last.then_inc(logits_done, 1)

            def turn_weights(a):
                pe.wait_ge(W_tok_ready, a + 1)
                pe.wait_ge(lg_ready, a + 1)
                mm(P0[0:NE * NB, 0:P], W_tok[:].rearrange("p n j -> p (n j)"), ident[:],
                   start=True, stop=True).then_inc(WT_done, 1)

            def turn_y(t, after):
                pe.wait_ge(yT_ready, t + 1)
                need(pe, x1_ready, after)
                if isinstance(t, int) and t == NT - 1:
                    pe.wait_ge(y_ready, t)
                for j in range(NB):
                    last = nc.tensor.transpose(P1[:, j * P:(j + 1) * P], yT[:, j * P:(j + 1) * P], ident[:])
                last.then_inc(OT_done, 1)

            def three(dst, w_hi, w_lo, m_hi, m_lo, start, stop):
                mm(dst, w_hi, m_hi, start=start, stop=False)
                mm(dst, w_hi, m_lo, start=False, stop=False)
                return mm(dst, w_lo, m_hi, start=False, stop=stop)

            def up(t, u, k):
                if k == 0:
                    pe.wait_ge(x_lo_ready, t + 1)
                need(pe, hid_ready, t * K + k - 1)
                sl = slice(k * P, (k + 1) * P)
                three(AB[:, k % 2, 0], W_hi[:, 0, sl], W_lo[:, 0, sl], x_hi[:, u], x_lo[:, u], True, True).then_inc(A_done, 1)
                three(AB[:, k % 2, 1], W_hi[:, 1, sl], W_lo[:, 1, sl], x_hi[:, u], x_lo[:, u], True, True).then_inc(B_done, 1)

            def down(t, k):
                pe.wait_ge(h_lo_ready, t * K + k + 1)
                if k == 0:
                    need(pe, yT_ready, t)
                sl = slice(k * E, (k + 1) * E)
                three(YB[:], W_hi[:, 2, sl], W_lo[:, 2, sl], h_hi[:, k % NH], h_lo[:, k % NH],
                      k == 0, k == K - 1).then_inc(Y_done, 1)

            def first_half(a):
                turn_x1(a)
                project_qk(a)
                project_v(a)
                fold_keys(a)
                score_global(a)
                score_windows(a)

            def macro(t, u, second, first):
                zero = isinstance(t, int) and t == 0
                for k in range(K):
                    if k + LEAD < K:
                        up(t, u, k + LEAD)
                    elif second:
                        up(t + 1, 1 - u, k + LEAD - K)
                    if second and k == 0:
                        turn_global_probs(t + 1)
                        window_context(t + 1)
                    if second and k == 1:
                        mix_global(t + 1)
                    if second and k == 2:
                        project_mix(t + 1)
                    if second and k == 3:
                        project_out(t + 1)
                    if first and k == 3:
                        turn_x1(t + 2)
                    if k == 4 and not zero:
                        turn_y(t - 1, t + 2 if second else NT)
                    if first and k == 4:
                        project_qk(t + 2)
                    if first and k == 5:
                        project_v(t + 2)
                        fold_keys(t + 2)
                    if second and k == 6:
                        turn_x2(t + 1, t + 3 if first else NT)
                    if second and k == 7:
                        score_experts(t + 1, 1 - u)
                    if first and k == 7:
                        score_global(t + 2)
                    if second and k == 9:
                        turn_weights(t + 1)
                    if first and k == 9:
                        score_windows(t + 2)
                    down(t, k)

            pe.wait_ge(ident_ready, 1)
            pe.wait_ge(small_in, 9 * 16)
            nc.tensor.transpose(P0[:, 0:P], Wk[:], ident[:]).then_inc(wkT_done, 1)
            pe.wait_ge(wkT_ready, 1)
            first_half(0)
            turn_global_probs(0)
            window_context(0)
            mix_global(0)
            project_mix(0)
            project_out(0)
            pe.wait_ge(w_lo_ready, 1)
            turn_x2(0, 1)
            score_experts(0, 0)
            turn_weights(0)
            pe.wait_ge(w_tile_ready, 1)
            first_half(1)
            pe.wait_ge(w_lo_ready, 4)
            for k in range(LEAD):
                up(0, 0, k)
            over_tiles(pe, macro)
            turn_y(NT - 1, NT)


_INS = ['L0_attn_hidden_states', 'L0_attn_Wq', 'L0_attn_bq', 'L0_attn_Wk', 'L0_attn_bk', 'L0_attn_Wv', 'L0_attn_bv',
        'L0_attn_Wo', 'L0_attn_bo', 'L0_ffn_gate_kernel', 'L0_ffn_w0_kernel', 'L0_ffn_w1_kernel', 'L0_ffn_wo_kernel']


def kernel(**inputs):
    import numpy as _np
    import concourse.bacc as _bacc
    from concourse import mybir as _mybir
    from concourse.bass_utils import run_bass_kernel_spmd as _run

    nc = _bacc.Bacc("TRN2", target_bir_lowering=False, num_devices=1)
    arrays, args = {}, []
    for name in _INS:
        a = _np.ascontiguousarray(inputs[name])
        arrays[f"in_{name}_dram"] = a
        args.append(nc.dram_tensor(f"in_{name}_dram", a.shape, _mybir.dt.from_np(a.dtype), kind="ExternalInput").ap())
    shape = tuple(inputs['L0_attn_hidden_states'].shape)
    args.append(nc.dram_tensor("out_0_dram", shape, _mybir.dt.float32, kind="ExternalOutput").ap())
    preln_attention_moe_kernel(nc, *args)
    r = _run(nc, [arrays], core_ids=[0])
    return r.results[0]["out_0_dram"]
```

```python
import concourse.bass as bass
from concourse import mybir
from contextlib import ExitStack


def preln_attention_moe_kernel(
    nc: bass.Bass,
    x: bass.AP,
    wq: bass.AP,
    bq: bass.AP,
    wk: bass.AP,
    bk: bass.AP,
    wv: bass.AP,
    bv: bass.AP,
    wo: bass.AP,
    bo: bass.AP,
    gate: bass.AP,
    w0: bass.AP,
    w1: bass.AP,
    w2: bass.AP,
    out: bass.AP,
):
    fp32 = mybir.dt.float32
    fp32r = mybir.dt.float32r
    u32 = mybir.dt.uint32
    ALU = mybir.AluOpType
    ACT = mybir.ActivationFunctionType
    AX = mybir.AxisListType

    NSEQ, SEQ, E = x.shape
    NE, _, H = w0.shape
    HEADS, D, WIN = 16, 8, 32
    SCALE = float(D) ** -0.5
    EPS = 1e-5
    P = 128
    NB = 4
    TOK = NB * P
    NT = NSEQ * SEQ // TOK
    NS = TOK // SEQ
    HC = H // P
    K = NE * HC
    LEAD = 4
    LAG = 2
    HG = HEADS // 4
    QC = WIN + 1
    GR = 32
    NH = 4
    NQ = 4

    x_v = x.rearrange("s l e -> (s l) e").rearrange("(t j p) e -> t p j e", j=NB, p=P)
    out_v = out.rearrange("s l e -> (s l) e").rearrange("(t j p) e -> t p j e", j=NB, p=P)
    w_rows = nc.dram_tensor("routing_rows", (NT, NE * TOK), fp32).ap()

    ctx = ExitStack()
    with ctx:
        def sb(name, shape, dt=fp32):
            return ctx.enter_context(nc.sbuf_tensor(name, shape, dt))

        def pb(name, shape, dt=fp32):
            return ctx.enter_context(nc.psum_tensor(name, shape, dt))

        def sem(name):
            return ctx.enter_context(nc.semaphore(name))

        ident = sb("ident", [P, P])
        head_mask = sb("head_mask", [P, GR])
        group_mask = sb("group_mask", [P, 4 * D])
        group_rows = sb("group_rows", [P, HG])
        in_group = sb("in_group", [P, 4])
        expert_no = sb("expert_no", [P, NE])
        half_power = sb("half_power", [P, NB])
        eps = sb("eps", [P, NB])
        idle = sb("idle", [P, 5])
        Wq, Wk, Wv, Wo, WkT = (sb(n, [P, E]) for n in ("Wq", "Wk", "Wv", "Wo", "WkT"))
        Bq, Bk, Bv = (sb(n, [P, 1]) for n in ("Bq", "Bk", "Bv"))
        Bo = sb("Bo", [P, E])
        G_in = sb("G_in", [P, NE])
        G_hi, G_lo = sb("G_hi", [P, NE], fp32r), sb("G_lo", [P, NE], fp32r)
        W2_in = sb("W2_in", [P, NE * H])
        W_hi, W_lo = sb("W_hi", [P, 3, NE * H], fp32r), sb("W_lo", [P, 3, NE * H], fp32r)

        X = sb("X", [P, NT * TOK])

        stats1, stats2 = sb("stats1", [P, NB, 6]), sb("stats2", [P, NB, 6])
        mv1, mv2 = sb("mv1", [P, NB, 2]), sb("mv2", [P, NB, 2])
        var1, var2 = sb("var1", [P, NB]), sb("var2", [P, NB])
        rstd1, rstd2 = sb("rstd1", [P, NB]), sb("rstd2", [P, NB])
        mr1, mr2 = sb("mr1", [P, NB]), sb("mr2", [P, NB])
        shift1, shift2 = sb("shift1", [P, NB]), sb("shift2", [P, NB])
        xn1, xn2 = sb("xn1", [P, 2, NB, E]), sb("xn2", [P, NB, E])
        xT = sb("xT", [P, TOK])
        xT_win = sb("xT_win", [P, NB, 4, WIN])
        QT, KT = sb("QT", [P, NB, QC]), sb("KT", [P, NB, WIN])
        q_glob = sb("q_glob", [P, NS, GR])
        q_heads = sb("q_heads", [P, NB, 4, WIN])
        k_groups = sb("k_groups", [P, NB, HG, WIN])
        v_heads = sb("v_heads", [P, NB, E])
        U, c_glob = sb("U", [P, NS * GR]), sb("c_glob", [NS * GR, 1])
        sg, pg = sb("sg", [NS * GR, SEQ]), sb("pg", [NS * GR, SEQ])
        pgn = sb("pgn", [NS * GR, SEQ])
        gmax, gshift, gsum, grec = (sb(n, [NS * GR, 1]) for n in ("gmax", "gshift", "gsum", "grec"))
        pgT = sb("pgT", [P, 2, NS * GR])
        gmix = sb("gmix", [P, NS * GR])
        zmask, zctx = sb("zmask", [P, NS, GR]), sb("zctx", [P, NS])
        wmax, wsum, wrec = (sb(n, [P, HG * NB]) for n in ("wmax", "wsum", "wrec"))
        ws, wp, wpn, wpT = (sb(n, [P, TOK]) for n in ("ws", "wp", "wpn", "wpT"))
        C = sb("C", [P, NB, QC])

        lg, top = sb("lg", [P, NB, NE]), sb("top", [P, NB, 8])
        top_no, top_nof = sb("top_no", [P, NB, 8], u32), sb("top_nof", [P, NB, 2])
        gap, tanh_gap = sb("gap", [P, NB]), sb("tanh_gap", [P, NB])
        share = sb("share", [P, 2, NB])
        pick = sb("pick", [P, 2, NE, NB])
        picked = sb("picked", [P, 2, NE, NB])
        W_tok = sb("W_tok", [P, NE, NB])
        w_tile = sb("w_tile", [NE * NB, P])

        Wb = sb("Wb", [P, 2, NE * TOK])
        W_in = [Wb[:, 1, 0:NE * H], Wb[:, 1, NE * H:2 * NE * H], W2_in[:]]
        x_hi, x_lo = sb("x_hi", [P, 2, TOK], fp32r), sb("x_lo", [P, 2, TOK], fp32r)
        sil, hid = sb("sil", [P, 2, TOK]), sb("hid", [P, NH, TOK])
        h_hi, h_lo = sb("h_hi", [P, NH, TOK], fp32r), sb("h_lo", [P, NH, TOK], fp32r)
        yT = sb("yT", [P, TOK])
        y_out = sb("y_out", [P, 2, NB, E])

        AB = pb("AB", [P, 2, 2, TOK])
        YB = pb("YB", [P, TOK])
        P0, P1, P2 = pb("P0", [P, TOK]), pb("P1", [P, TOK]), pb("P2", [P, TOK])

        x_in = [sem("x_in0"), sem("x_in1")]
        small_in, moe_in = sem("small_in"), sem("moe_in")
        consts_ready, ident_ready, wkT_done, wkT_ready = (
            sem(n) for n in ("consts_ready", "ident_ready", "wkT_done", "wkT_ready"))
        w_hi_ready, w_lo_ready = sem("w_hi_ready"), sem("w_lo_ready")
        (stats1_ready, scale1_ready, xn1_ready, T1_done, xT_ready, QK_done, QT_ready, KT_ready,
         q_glob_ready, qk_spread, U_done, U_ready, V_done, v_heads_ready, G_done, sg_ready,
         pg_ready, pgn_ready, S_done, ws_ready, wp_ready, wrec_ready, wpn_ready, wpT_ready,
         pgT_done, pgT_ready, mix_done, gmix_ready, Z_done, zctx_ready, CT_done, C_ready,
         O_done, bo_added, x1_ready, stats2_ready, scale2_ready, xn2_ready, T2_done, x_hi_ready,
         x_lo_ready, logits_done, lg_ready, gap_ready, tanh_ready, share_ready, W_tok_ready,
         WT_done, w_tile_ready) = (
            sem(n) for n in (
                "stats1_ready", "scale1_ready", "xn1_ready", "T1_done", "xT_ready", "QK_done",
                "QT_ready", "KT_ready", "q_glob_ready", "qk_spread", "U_done", "U_ready",
                "V_done", "v_heads_ready", "G_done", "sg_ready", "pg_ready", "pgn_ready",
                "S_done", "ws_ready", "wp_ready", "wrec_ready", "wpn_ready", "wpT_ready",
                "pgT_done", "pgT_ready", "mix_done", "gmix_ready", "Z_done", "zctx_ready",
                "CT_done", "C_ready", "O_done", "bo_added", "x1_ready", "stats2_ready",
                "scale2_ready", "xn2_ready", "T2_done", "x_hi_ready", "x_lo_ready",
                "logits_done", "lg_ready", "gap_ready", "tanh_ready", "share_ready",
                "W_tok_ready", "WT_done", "w_tile_ready"))
        rows_out = sem("rows_out")
        wb_in = [sem(f"wb_in{q}") for q in range(NQ)]
        A_done, B_done, sil_ready, prod_ready, hid_ready, h_hi_ready, h_lo_ready, Y_done = (
            sem(n) for n in ("A_done", "B_done", "sil_ready", "prod_ready", "hid_ready",
                             "h_hi_ready", "h_lo_ready", "Y_done"))
        yT_ready, OT_done, y_ready = sem("yT_ready"), sem("OT_done"), sem("y_ready")
        stored = [sem("stored0"), sem("stored1")]

        def need(eng, s, n):
            if not (isinstance(n, int) and n <= 0):
                eng.wait_ge(s, n)

        def tile_of(X_, a, rows=P):
            return X_[0:rows, bass.ds(a * TOK, TOK)]

        def has(a):
            return not isinstance(a, int) or 0 <= a < NT

        def most(a):
            return min(a, NT) if isinstance(a, int) else a

        def over_tiles(eng, macro):
            for t in range(-3, 1):
                macro(t, t % 2)
            with eng.Fori(0, (NT - 4) // 2, 1) as i:
                macro(i * 2 + 1, 1)
                macro(i * 2 + 2, 0)
            for t in range(NT - 3, NT):
                macro(t, t % 2)

        block = ctx.enter_context(nc.Block())

        @block.sync
        def _(sp):
            def load_x(a, u):
                need(sp, x_in[u], (a - u) // 2 * 16 if isinstance(a, int) else (a - u) * 8)
                sp.dma_start(tile_of(X, a).rearrange("p (j e) -> p j e", j=NB),
                             x_v[bass.ds(a, 1)].rearrange("a p j e -> (a p) j e")
                             if not isinstance(a, int) else x_v[a]).then_inc(x_in[u], 16)

            load_x(0, 0)
            for dst, src in ((Wq, wq), (Wk, wk), (Wv, wv), (Wo, wo), (G_in, gate)):
                sp.dma_start(dst[:], src).then_inc(small_in, 16)
            for dst, src in ((Bq, bq), (Bk, bk), (Bv, bv)):
                sp.dma_start(dst[:], src.rearrange("(p o) -> p o", o=1)).then_inc(small_in, 16)
            sp.dma_start(Bo[:], bo.rearrange("(o e) -> o e", o=1).broadcast_to([P, E])).then_inc(small_in, 16)
            load_x(1, 1)
            with sp.Fori(1, NT // 2, 1) as i:
                load_x(i * 2, 0)
                load_x(i * 2 + 1, 1)

            def spread_routing(a, u):
                if isinstance(a, int) and a == 1:
                    sp.wait_ge(w_lo_ready, 4)
                sp.wait_ge(w_tile_ready, a + 1)
                sp.dma_start(w_rows[bass.ds(a, 1)].rearrange("o (r p) -> (o r) p", p=P), w_tile[:]).then_inc(rows_out, 16)
                sp.wait_ge(rows_out, a * 16 + 16)
                part = NE * TOK // NQ
                for q in range(NQ):
                    sp.dma_start(Wb[:, u, q * part:(q + 1) * part],
                                 w_rows[bass.ds(a, 1), q * part:(q + 1) * part].broadcast_to([P, part])).then_inc(wb_in[q], 16)

            def store(t, u):
                sp.wait_ge(y_ready, t + 1)
                dst = out_v[t] if isinstance(t, int) else out_v[bass.ds(t, 1)].rearrange("a p j e -> (a p) j e")
                sp.dma_start(dst, y_out[:, u]).then_inc(stored[u], 16)

            def macro(t, u):
                if has(t - 1):
                    store(t - 1, 1 - u)
                if has(t + 1):
                    spread_routing(t + 1, 1 - u)

            over_tiles(sp, macro)
            store(NT - 1, (NT - 1) % 2)
            for u in range(2):
                sp.wait_ge(stored[u], NT // 2 * 16)

        @block.gpsimd
        def _(pool):
            g = nc.gpsimd
            g.memset(ident[:], 0.0)
            g.memset(head_mask[:], 1.0)
            g.memset(group_mask[:], 1.0)
            g.memset(half_power[:], -0.5)
            g.memset(eps[:], EPS)
            g.memset(C[:], 0.0)
            for n in range(NE):
                g.memset(expert_no[:, n:n + 1], float(n))
            pool.drain()
            g.affine_select(out=ident[:], in_=ident[:], compare_op=ALU.not_equal, fill=1.0, base=0,
                            pattern=[[-1, P]], channel_multiplier=1).then_inc(ident_ready, 1)
            g.affine_select(out=head_mask[:], in_=head_mask[:], compare_op=ALU.is_ge, fill=0.0, base=0,
                            pattern=[[-D, GR]], channel_multiplier=1)
            gm = group_mask[:].rearrange("p (g d) -> p g d", d=D)
            g.affine_select(out=gm, in_=gm, compare_op=ALU.is_ge, fill=0.0, base=0,
                            pattern=[[-WIN, 4], [0, D]], channel_multiplier=1)
            pool.drain()
            g.affine_select(out=head_mask[:], in_=head_mask[:], compare_op=ALU.is_ge, fill=0.0, base=D - 1,
                            pattern=[[D, GR]], channel_multiplier=-1)
            g.affine_select(out=gm, in_=gm, compare_op=ALU.is_ge, fill=0.0, base=WIN - 1,
                            pattern=[[WIN, 4], [0, D]], channel_multiplier=-1).then_inc(consts_ready, 1)
            pool.drain()
            g.tensor_tensor(in_group[:], head_mask[:, 0:4], head_mask[:, 4:8], ALU.add)
            pool.drain()
            g.tensor_tensor(in_group[:], in_group[:], head_mask[:, 8:12], ALU.add)
            pool.drain()
            g.tensor_tensor(in_group[:], in_group[:], head_mask[:, 12:16], ALU.add)
            g.memset(group_rows[:], 1.0)
            pool.drain()
            g.affine_select(out=group_rows[:], in_=group_rows[:], compare_op=ALU.is_ge, fill=0.0, base=0,
                            pattern=[[-4 * D, HG]], channel_multiplier=1)
            pool.drain()
            g.affine_select(out=group_rows[:], in_=group_rows[:], compare_op=ALU.is_ge, fill=0.0, base=4 * D - 1,
                            pattern=[[4 * D, HG]], channel_multiplier=-1)
            pool.drain()

            def norm_scale(a, stats_ready, mv, var, rstd, mr, shift, used, ready):
                pool.wait_ge(stats_ready, a + 1)
                need(pool, used, a)
                g.tensor_tensor(var[:], mv[:, :, 1], eps[:], ALU.add)
                pool.drain()
                g.tensor_tensor(rstd[:], var[:], half_power[:], ALU.pow)
                pool.drain()
                g.tensor_tensor(mr[:], mv[:, :, 0], rstd[:], ALU.mult)
                pool.drain()
                g.tensor_scalar(shift[:], mr[:], -1.0, None, ALU.mult).then_inc(ready, 1)

            def scale1(a):
                norm_scale(a, stats1_ready, mv1, var1, rstd1, mr1, shift1, xn1_ready, scale1_ready)

            def scale2(a):
                norm_scale(a, stats2_ready, mv2, var2, rstd2, mr2, shift2, xn2_ready, scale2_ready)

            def spread_q_glob(a):
                pool.wait_ge(QT_ready, a + 1)
                need(pool, U_done, a)
                g.tensor_tensor(q_glob[:], QT[:, 0:NB:2, 0:1].broadcast_to([P, NS, GR]),
                                head_mask[:].unsqueeze(1).broadcast_to([P, NS, GR]), ALU.mult).then_inc(q_glob_ready, 1)

            def spread_q(a):
                need(pool, S_done, a)
                g.tensor_tensor(q_heads[:], QT[:, :, 1:QC].unsqueeze(2).broadcast_to([P, NB, 4, WIN]),
                                in_group[:].unsqueeze(1).unsqueeze(3).broadcast_to([P, NB, 4, WIN]), ALU.mult)

            def spread_k(a):
                pool.wait_ge(KT_ready, a + 1)
                g.tensor_tensor(k_groups[:], KT[:].unsqueeze(2).broadcast_to([P, NB, HG, WIN]),
                                group_rows[:].unsqueeze(1).unsqueeze(3).broadcast_to([P, NB, HG, WIN]),
                                ALU.mult).then_inc(qk_spread, 1)

            def add_bo(a):
                pool.wait_ge(xn1_ready, a + 1)
                xt = tile_of(X, a).rearrange("p (j e) -> p j e", j=NB)
                g.tensor_tensor(xt, xt, Bo[:].unsqueeze(1).broadcast_to([P, NB, E]), ALU.add).then_inc(bo_added, 1)

            def window_probs(a):
                pool.wait_ge(wrec_ready, a + 1)
                need(pool, wpT_ready, a)
                g.tensor_tensor(wpn[:].rearrange("p (b k) -> p b k", k=WIN), wp[:].rearrange("p (b k) -> p b k", k=WIN),
                                wrec[:].unsqueeze(2).broadcast_to([P, HG * NB, WIN]), ALU.mult).then_inc(wpn_ready, 1)

            def token_weights(a):
                pool.wait_ge(share_ready, a + 1)
                need(pool, WT_done, a)
                g.tensor_tensor(picked[:], pick[:], share[:].unsqueeze(2).broadcast_to([P, 2, NE, NB]), ALU.mult)
                pool.drain()
                g.tensor_tensor(W_tok[:], picked[:, 0], picked[:, 1], ALU.add).then_inc(W_tok_ready, 1)

            def weight(t, u, k):
                if k % (K // NQ) == 0:
                    pool.wait_ge(wb_in[k // (K // NQ)], t * 16 + 16)
                pool.wait_ge(prod_ready, t * K + k + 1)
                n = k // HC
                h = hid[:, k % NH]
                g.tensor_tensor(h, h, Wb[:, u, n * TOK:(n + 1) * TOK], ALU.mult).then_inc(hid_ready, 1)

            def macro(t, u):
                for k in range(K):
                    if has(t):
                        weight(t, u, k)
                    if k == 6 and has(t + 3):
                        scale1(t + 3)
                    if k == 4 and has(t + 2):
                        window_probs(t + 2)
                    if k == 8 and has(t + 2):
                        add_bo(t + 2)
                    if k == 11 and has(t + 3):
                        spread_q_glob(t + 3)
                    if k == 11 and has(t + 1):
                        token_weights(t + 1)
                    if k == 12 and has(t + 3):
                        spread_q(t + 3)
                    if k == 13 and has(t + 3):
                        spread_k(t + 3)
                    if k == 14 and has(t + 2):
                        scale2(t + 2)

            pool.wait_ge(small_in, 9 * 16)
            over_tiles(pool, macro)

        @block.scalar
        def _(act):
            s = nc.scalar

            def normalise1(a, u, j):
                if j == 0:
                    act.wait_ge(scale1_ready, a + 1)
                    need(act, mix_done, a - 1)
                    s.activation(idle[:, 0:1], rstd1[:, 0:1], ACT.Copy)
                ins = s.activation(xn1[:, u, j], X[:, bass.ds(a * TOK + j * E, E)], ACT.Identity,
                                   scale=rstd1[:, j:j + 1], bias=shift1[:, j:j + 1])
                if j == NB - 1:
                    ins.then_inc(xn1_ready, 1)

            def keep_xT(a):
                act.wait_ge(T1_done, a + 1)
                need(act, G_done, a)
                s.activation(xT[:], P0[:], ACT.Identity)
                win = P0[:].rearrange("p (j q) -> p j q", q=P)[:, :, 1:QC]
                s.activation(xT_win[:], win.unsqueeze(2).broadcast_to([P, NB, 4, WIN]), ACT.Identity).then_inc(xT_ready, 1)

            def keep_qk(a):
                act.wait_ge(QK_done, a + 1)
                need(act, qk_spread, a)
                nq = NB * QC
                s.activation(QT[:], P0[:, 0:nq].rearrange("p (j q) -> p j q", q=QC), ACT.Identity,
                             bias=Bq[:, 0:1]).then_inc(QT_ready, 1)
                s.activation(KT[:], P0[:, nq:nq + NB * WIN].rearrange("p (j q) -> p j q", q=WIN), ACT.Identity,
                             bias=Bk[:, 0:1]).then_inc(KT_ready, 1)

            def keep_U(a):
                act.wait_ge(U_done, a + 1)
                need(act, sg_ready, a)
                s.activation(c_glob[:], P1[0:NS * GR, NS * GR:NS * GR + 1], ACT.Identity)
                s.activation(U[:], P1[:, 0:NS * GR], ACT.Identity).then_inc(U_ready, 1)

            def exps(a):
                act.wait_ge(sg_ready, a + 1)
                need(act, pgn_ready, a)
                s.activation(pg[:], sg[:], ACT.Exp, scale=SCALE, bias=gshift[:, 0:1],
                             accum_out=gsum[:, 0:1]).then_inc(pg_ready, 1)
                act.wait_ge(ws_ready, a + 1)
                need(act, wpn_ready, a)
                s.activation(wp[:], ws[:], ACT.Exp, scale=SCALE).then_inc(wp_ready, 1)

            def keep_context(a):
                act.wait_ge(CT_done, a + 1)
                need(act, O_done, a)
                s.activation(C[:, :, 1:QC], P1[:, 0:NB * WIN].rearrange("p (j q) -> p j q", q=WIN), ACT.Identity,
                             bias=Bv[:, 0:1]).then_inc(C_ready, 1)

            def split_x(a, u):
                act.wait_ge(T2_done, a + 1)
                need(act, B_done, a * K - K)
                s.activation(x_hi[:, u], P0[:], ACT.Copy).then_inc(x_hi_ready, 1)

            def keep_logits(a):
                act.wait_ge(logits_done, a + 1)
                need(act, share_ready, a)
                s.activation(lg[:], P0[:, 0:NB * NE].rearrange("p (j n) -> p j n", n=NE), ACT.Copy).then_inc(lg_ready, 1)

            def tanh(a):
                act.wait_ge(gap_ready, a + 1)
                s.activation(tanh_gap[:], gap[:], ACT.Tanh, scale=0.5).then_inc(tanh_ready, 1)

            def keep_w_tile(a):
                act.wait_ge(WT_done, a + 1)
                need(act, rows_out, a * 16)
                s.activation(w_tile[:], P2[0:NE * NB, 0:P], ACT.Copy).then_inc(w_tile_ready, 1)

            def silu(t, k):
                act.wait_ge(A_done, t * K + k + 1)
                need(act, prod_ready, t * K + k - 1)
                s.activation(sil[:, k % 2], AB[:, k % 2, 0], ACT.Silu).then_inc(sil_ready, 1)

            def split_h(t, k):
                act.wait_ge(hid_ready, t * K + k + 1)
                need(act, Y_done, t * K + k - NH + 1)
                s.activation(h_hi[:, k % NH], hid[:, k % NH], ACT.Copy).then_inc(h_hi_ready, 1)

            def split_weights(m):
                s.activation(W_hi[:, m], W_in[m], ACT.Copy).then_inc(w_hi_ready, 1)

            def macro(t, u):
                for k in range(K):
                    if has(t):
                        silu(t, k)
                    if k == 3 and has(t + 2):
                        exps(t + 2)
                    if k >= LAG and has(t):
                        split_h(t, k - LAG)
                    if k < LAG and has(t - 1):
                        split_h(t - 1, K + k - LAG)
                    if k == 1 and isinstance(t, int) and t == -2:
                        act.wait_ge(moe_in, 3 * 16)
                        for m in range(3):
                            split_weights(m)
                    if k in (7, 8) and has(t + 3):
                        for j in range(2 * (k - 7), 2 * (k - 6)):
                            normalise1(t + 3, 1 - u, j)
                    if k == 4 and has(t + 1):
                        split_x(t + 1, 1 - u)
                    if k == 8 and has(t + 1):
                        keep_logits(t + 1)
                    if k == 10 and has(t + 2):
                        keep_context(t + 2)
                    if k == 9 and has(t + 3):
                        keep_xT(t + 3)
                    if k == 11 and has(t + 3):
                        keep_qk(t + 3)
                    if k == 10 and has(t + 1):
                        tanh(t + 1)
                    if k == 14 and has(t + 3):
                        keep_U(t + 3)
                    if k == 14 and has(t + 1):
                        keep_w_tile(t + 1)

            act.dma_start(W_in[0].rearrange("p (n h) -> p n h", n=NE), w0.rearrange("n e h -> e n h")).then_inc(moe_in, 16)
            act.dma_start(W_in[1].rearrange("p (n h) -> p n h", n=NE), w1.rearrange("n e h -> e n h")).then_inc(moe_in, 16)
            act.dma_start(W_in[2].rearrange("p (n e) -> p n e", e=E), w2.rearrange("n (c p) e -> p (n c) e", p=P)).then_inc(moe_in, 16)
            act.wait_ge(small_in, 9 * 16)
            act.wait_ge(consts_ready, 1)
            act.wait_ge(wkT_done, 1)
            s.activation(WkT[:], P0[:, 0:P], ACT.Identity).then_inc(wkT_ready, 1)
            s.activation(G_hi[:], G_in[:], ACT.Copy).then_inc(w_hi_ready, 1)
            over_tiles(act, macro)
            for k in range(K - LAG, K):
                split_h(NT - 1, k)

        @block.vector
        def _(dve):
            v = nc.vector

            def statistics(a, stats, mv, used, ready, spare):
                need(dve, used, a)
                v.memset(idle[:, spare:spare + 1], 0.0)
                for j in range(NB):
                    v.bn_stats(stats[:, j], X[:, bass.ds(a * TOK + j * E, E)])
                dve.drain()
                for j in range(NB):
                    last = v.bn_aggr(mv[:, j], stats[:, j])
                last.then_inc(ready, 1)

            def statistics1(a, u):
                dve.wait_ge(x_in[u], (a - u) // 2 * 16 + 16 if isinstance(a, int) else (a - u) * 8 + 16)
                statistics(a, stats1, mv1, scale1_ready, stats1_ready, 2)

            def statistics2(a):
                dve.wait_ge(x1_ready, a + 1)
                statistics(a, stats2, mv2, scale2_ready, stats2_ready, 3)

            def normalise2(a):
                dve.wait_ge(scale2_ready, a + 1)
                need(dve, T2_done, a)
                v.memset(idle[:, 1:2], 0.0)
                for j in range(NB):
                    last = v.tensor_scalar(xn2[:, j], X[:, bass.ds(a * TOK + j * E, E)],
                                           rstd2[:, j:j + 1], shift2[:, j:j + 1], ALU.mult, ALU.add)
                last.then_inc(xn2_ready, 1)

            def spread_v(a):
                dve.wait_ge(V_done, a + 1)
                need(dve, CT_done, a)
                v.tensor_tensor(v_heads[:].rearrange("p w (c m) -> p (w c) m", m=4 * D),
                                P1[:].rearrange("p (b m) -> p b m", m=4 * D),
                                group_mask[:].unsqueeze(1).broadcast_to([P, HG * NB, 4 * D]), ALU.mult).then_inc(v_heads_ready, 1)

            def global_scores(a):
                dve.wait_ge(G_done, a + 1)
                dve.wait_ge(U_ready, a + 1)
                need(dve, pg_ready, a)
                v.tensor_scalar(sg[:], P2[0:NS * GR, 0:SEQ], c_glob[:, 0:1], None, ALU.add)
                dve.drain()
                v.tensor_reduce(gmax[:], sg[:], AX.X, ALU.max)
                dve.drain()
                v.tensor_scalar(gshift[:], gmax[:], -SCALE, None, ALU.mult).then_inc(sg_ready, 1)

            def window_scores(a):
                dve.wait_ge(S_done, a + 1)
                need(dve, wp_ready, a)
                sc = P1[:].rearrange("p (b k) -> p b k", k=WIN)
                v.tensor_reduce(wmax[:], sc, AX.X, ALU.max)
                dve.drain()
                v.tensor_tensor(ws[:].rearrange("p (b k) -> p b k", k=WIN), sc,
                                wmax[:].unsqueeze(2).broadcast_to([P, HG * NB, WIN]), ALU.subtract).then_inc(ws_ready, 1)

            def global_probs(a):
                dve.wait_ge(pg_ready, a + 1)
                need(dve, pgT_done, a)
                v.reciprocal(grec[:], gsum[:])
                dve.drain()
                v.tensor_scalar(pgn[:], pg[:], grec[:, 0:1], None, ALU.mult).then_inc(pgn_ready, 1)

            def window_sums(a):
                dve.wait_ge(wp_ready, a + 1)
                need(dve, wpn_ready, a)
                v.tensor_reduce(wsum[:], wp[:].rearrange("p (b k) -> p b k", k=WIN), AX.X, ALU.add)
                dve.drain()
                v.reciprocal(wrec[:], wsum[:]).then_inc(wrec_ready, 1)

            def turn_probs(a):
                dve.wait_ge(wpn_ready, a + 1)
                need(dve, CT_done, a)
                v.transpose(wpT[:], wpn[:]).then_inc(wpT_ready, 1)

            def keep_pgT(a):
                dve.wait_ge(pgT_done, a + 1)
                need(dve, mix_done, a)
                v.tensor_copy(pgT[:], P2[:, 0:2 * NS * GR].rearrange("p (c r) -> p c r", c=2)).then_inc(pgT_ready, 1)

            def keep_mix(a):
                dve.wait_ge(mix_done, a + 1)
                need(dve, Z_done, a)
                v.tensor_copy(gmix[:], P2[:, 0:NS * GR]).then_inc(gmix_ready, 1)

            def global_context(a):
                dve.wait_ge(Z_done, a + 1)
                need(dve, O_done, a)
                v.tensor_tensor(zmask[:], P2[:, 0:NS * GR].rearrange("p (s h) -> p s h", s=NS),
                                head_mask[:].unsqueeze(1).broadcast_to([P, NS, GR]), ALU.mult)
                dve.drain()
                v.tensor_reduce(zctx[:], zmask[:], AX.X, ALU.add)
                dve.drain()
                v.tensor_scalar(C[:, 0:NB:2, 0], zctx[:], Bv[:, 0:1], None, ALU.add).then_inc(zctx_ready, 1)

            def add_attention(a):
                dve.wait_ge(O_done, a + 1)
                dve.wait_ge(bo_added, a + 1)
                xt = tile_of(X, a, QC)
                v.tensor_tensor(xt, xt, P0[0:QC, :], ALU.add).then_inc(x1_ready, 1)

            def rest_x(a, u):
                dve.wait_ge(x_hi_ready, a + 1)
                need(dve, B_done, a * K - K)
                v.tensor_tensor(x_lo[:, u], P0[:], x_hi[:, u], ALU.subtract).then_inc(x_lo_ready, 1)

            def top_two(a):
                dve.wait_ge(lg_ready, a + 1)
                need(dve, W_tok_ready, a)
                v.memset(idle[:, 4:5], 0.0)
                for j in range(NB):
                    v.max(top[:, j], lg[:, j])
                dve.drain()
                v.tensor_tensor(gap[:], top[:, :, 0], top[:, :, 1], ALU.subtract).then_inc(gap_ready, 1)
                for j in range(NB):
                    v.max_index(top_no[:, j], top[:, j], lg[:, j])
                dve.drain()
                v.tensor_copy(top_nof[:], top_no[:, :, 0:2])
                dve.drain()
                for r in range(2):
                    v.tensor_tensor(pick[:, r], expert_no[:].unsqueeze(2).broadcast_to([P, NE, NB]),
                                    top_nof[:, :, r].unsqueeze(1).broadcast_to([P, NE, NB]), ALU.is_equal)

            def shares(a):
                dve.wait_ge(tanh_ready, a + 1)
                v.tensor_scalar(share[:, 0], tanh_gap[:], 0.5, 0.5, ALU.mult, ALU.add)
                v.tensor_scalar(share[:, 1], tanh_gap[:], -0.5, 0.5, ALU.mult, ALU.add).then_inc(share_ready, 1)

            def product(t, k):
                dve.wait_ge(sil_ready, t * K + k + 1)
                dve.wait_ge(B_done, t * K + k + 1)
                need(dve, h_lo_ready, t * K + k - NH + 1)
                v.tensor_tensor(hid[:, k % NH], sil[:, k % 2], AB[:, k % 2, 1], ALU.mult).then_inc(prod_ready, 1)

            def rest_h(t, k):
                dve.wait_ge(h_hi_ready, t * K + k + 1)
                v.tensor_tensor(h_lo[:, k % NH], hid[:, k % NH], h_hi[:, k % NH], ALU.subtract).then_inc(h_lo_ready, 1)

            def keep_y(t):
                dve.wait_ge(Y_done, t * K + K)
                need(dve, OT_done, t)
                v.tensor_copy(yT[:], YB[:]).then_inc(yT_ready, 1)

            def finish(t, u):
                dve.wait_ge(OT_done, t + 1)
                need(dve, stored[u], (t - u) // 2 * 16 if isinstance(t, int) else (t - u) * 8)
                v.tensor_tensor(y_out[:, u].rearrange("p j e -> p (j e)"), P1[:], tile_of(X, t), ALU.add).then_inc(y_ready, 1)

            def macro(t, u):
                for k in range(K):
                    if has(t):
                        product(t, k)
                        if k >= LAG:
                            rest_h(t, k - LAG)
                    if k < LAG and has(t - 1):
                        rest_h(t - 1, K + k - LAG)
                    if k == 0 and has(t + 1):
                        normalise2(t + 1)
                    if k == 1 and has(t + 2):
                        global_scores(t + 2)
                    if k == 2 and has(t - 1):
                        keep_y(t - 1)
                    if k == 5 and has(t + 3):
                        statistics1(t + 3, 1 - u)
                    if k == 3 and has(t + 2):
                        window_sums(t + 2)
                    if k == 4 and has(t + 2):
                        global_probs(t + 2)
                    if k == 4 and has(t + 1):
                        rest_x(t + 1, 1 - u)
                    if k == 6 and has(t + 2):
                        turn_probs(t + 2)
                    if k == 7 and has(t + 2):
                        keep_pgT(t + 2)
                    if k == 7 and has(t - 1):
                        finish(t - 1, 1 - u)
                    if k in (1, 2, 3) and isinstance(t, int) and t == -2:
                        rest_weights(k - 1)
                    if k == 9 and has(t + 2):
                        keep_mix(t + 2)
                    if k == 9 and has(t + 1):
                        top_two(t + 1)
                    if k == 11 and has(t + 3):
                        spread_v(t + 3)
                    if k == 11 and has(t + 1):
                        shares(t + 1)
                    if k == 11 and has(t + 2):
                        global_context(t + 2)
                    if k == 13 and has(t + 2):
                        add_attention(t + 2)
                    if k == 14 and has(t + 2):
                        statistics2(t + 2)
                    if k == 15 and has(t + 3):
                        window_scores(t + 3)

            def rest_weights(m):
                dve.wait_ge(w_hi_ready, m + 2)
                v.tensor_tensor(W_lo[:, m], W_in[m], W_hi[:, m], ALU.subtract).then_inc(w_lo_ready, 1)

            dve.wait_ge(consts_ready, 1)
            dve.wait_ge(w_hi_ready, 1)
            v.tensor_tensor(G_lo[:], G_in[:], G_hi[:], ALU.subtract).then_inc(w_lo_ready, 1)
            over_tiles(dve, macro)
            for k in range(K - LAG, K):
                rest_h(NT - 1, k)
            keep_y(NT - 1)
            finish(NT - 1, (NT - 1) % 2)

        @block.tensor
        def _(pe):
            mm = nc.tensor.matmul

            def turn_x1(a, u):
                pe.wait_ge(xn1_ready, a + 1)
                need(pe, lg_ready, a - 1)
                for j in range(NB):
                    last = nc.tensor.transpose(P0[:, j * P:(j + 1) * P], xn1[:, u, j], ident[:])
                last.then_inc(T1_done, 1)

            def project_qk(a):
                pe.wait_ge(xT_ready, a + 1)
                xw = xT[:].rearrange("p (j q) -> p j q", q=P)
                nq = NB * QC
                mm(P0[:, 0:nq], Wq[:], xw[:, :, 0:QC], start=True, stop=True)
                mm(P0[:, nq:nq + NB * WIN], Wk[:], xw[:, :, 1:QC], start=True, stop=True).then_inc(QK_done, 1)

            def project_v(a):
                pe.wait_ge(xT_ready, a + 1)
                need(pe, C_ready, a)
                for w in range(NB):
                    last = mm(P1[:, w * E:(w + 1) * E], xT_win[:, w].rearrange("p r k -> p (r k)"), Wv[:], start=True, stop=True)
                last.then_inc(V_done, 1)

            def fold_keys(a):
                pe.wait_ge(q_glob_ready, a + 1)
                pe.wait_ge(v_heads_ready, a + 1)
                qg = q_glob[:].rearrange("p s h -> p (s h)")
                mm(P1[:, 0:NS * GR], WkT[:], qg, start=True, stop=True)
                mm(P1[0:NS * GR, NS * GR:NS * GR + 1], qg, Bk[:], start=True, stop=True).then_inc(U_done, 1)

            def score_global(a):
                pe.wait_ge(U_ready, a + 1)
                need(pe, w_tile_ready, a - 1)
                if isinstance(a, int) and a < 2:
                    need(pe, zctx_ready, a)
                for b in range(NS):
                    last = mm(P2[b * GR:(b + 1) * GR, 0:SEQ], U[:, b * GR:(b + 1) * GR],
                              xT[:, b * SEQ:(b + 1) * SEQ], start=True, stop=True)
                last.then_inc(G_done, 1)

            def score_windows(a):
                pe.wait_ge(qk_spread, a + 1)
                pe.wait_ge(U_ready, a + 1)
                for w in range(NB):
                    last = mm(P1[:, w * P:(w + 1) * P], q_heads[:, w].rearrange("p g q -> p (g q)"),
                              k_groups[:, w].rearrange("p c k -> p (c k)"), start=True, stop=True)
                last.then_inc(S_done, 1)

            def turn_global_probs(a):
                pe.wait_ge(pgn_ready, a + 1)
                pe.wait_ge(sg_ready, a + 1)
                r = NS * GR
                for c in range(SEQ // P):
                    last = mm(P2[:, c * r:(c + 1) * r], pgn[:, c * P:(c + 1) * P], ident[0:r, 0:r], start=True, stop=True)
                last.then_inc(pgT_done, 1)

            def mix_global(a, u):
                pe.wait_ge(pgT_ready, a + 1)
                for b in range(NS):
                    for c in range(SEQ // P):
                        last = mm(P2[:, b * GR:(b + 1) * GR], xn1[:, u, b * 2 + c], pgT[:, c, b * GR:(b + 1) * GR],
                                  start=(c == 0), stop=(c == SEQ // P - 1))
                last.then_inc(mix_done, 1)

            def project_mix(a):
                pe.wait_ge(gmix_ready, a + 1)
                mm(P2[:, 0:NS * GR], Wv[:], gmix[:], start=True, stop=True).then_inc(Z_done, 1)

            def window_context(a):
                pe.wait_ge(wpT_ready, a + 1)
                pe.wait_ge(v_heads_ready, a + 1)
                need(pe, y_ready, a - 2)
                for w in range(NB):
                    for c in range(HG):
                        col = (w * HG + c) * WIN
                        last = mm(P1[32 * c:32 * (c + 1), w * WIN:(w + 1) * WIN], v_heads[:, w, 32 * c:32 * (c + 1)],
                                  wpT[:, col:col + WIN], start=True, stop=True)
                last.then_inc(CT_done, 1)

            def project_out(a):
                pe.wait_ge(C_ready, a + 1)
                pe.wait_ge(zctx_ready, a + 1)
                pe.wait_ge(KT_ready, most(a + 2))
                for j in range(NB):
                    last = mm(P0[0:QC, j * E:(j + 1) * E], C[:, j], Wo[:], start=True, stop=True)
                last.then_inc(O_done, 1)

            def turn_x2(a):
                pe.wait_ge(xn2_ready, a + 1)
                for j in range(NB):
                    last = nc.tensor.transpose(P0[:, j * P:(j + 1) * P], xn2[:, j], ident[:])
                last.then_inc(T2_done, 1)

            def score_experts(a, u):
                pe.wait_ge(x_lo_ready, a + 1)
                for j in range(NB):
                    sl = slice(j * P, (j + 1) * P)
                    dst = P0[:, j * NE:(j + 1) * NE]
                    mm(dst, x_hi[:, u, sl], G_hi[:], start=True, stop=False)
                    mm(dst, x_hi[:, u, sl], G_lo[:], start=False, stop=False)
                    last = mm(dst, x_lo[:, u, sl], G_hi[:], start=False, stop=True)
                last.then_inc(logits_done, 1)

            def turn_weights(a):
                pe.wait_ge(W_tok_ready, a + 1)
                pe.wait_ge(zctx_ready, most(a + 2))
                mm(P2[0:NE * NB, 0:P], W_tok[:].rearrange("p n j -> p (n j)"), ident[:],
                   start=True, stop=True).then_inc(WT_done, 1)

            def turn_y(t):
                pe.wait_ge(yT_ready, t + 1)
                pe.wait_ge(ws_ready, most(t + 4))
                if isinstance(t, int):
                    pe.wait_ge(C_ready, most(t + 3))
                    need(pe, y_ready, t)
                for j in range(NB):
                    last = nc.tensor.transpose(P1[:, j * P:(j + 1) * P], yT[:, j * P:(j + 1) * P], ident[:])
                last.then_inc(OT_done, 1)

            def three(dst, w_hi, w_lo, m_hi, m_lo, start, stop):
                mm(dst, w_hi, m_hi, start=start, stop=False)
                mm(dst, w_hi, m_lo, start=False, stop=False)
                return mm(dst, w_lo, m_hi, start=False, stop=stop)

            def up(t, u, k):
                if k == 0:
                    pe.wait_ge(x_lo_ready, t + 1)
                    if isinstance(t, int) and t == 0:
                        pe.wait_ge(w_lo_ready, 4)
                need(pe, prod_ready, t * K + k - 1)
                sl = slice(k * P, (k + 1) * P)
                three(AB[:, k % 2, 0], W_hi[:, 0, sl], W_lo[:, 0, sl], x_hi[:, u], x_lo[:, u], True, True).then_inc(A_done, 1)
                three(AB[:, k % 2, 1], W_hi[:, 1, sl], W_lo[:, 1, sl], x_hi[:, u], x_lo[:, u], True, True).then_inc(B_done, 1)

            def down(t, k):
                pe.wait_ge(h_lo_ready, t * K + k + 1)
                if k == 0:
                    need(pe, yT_ready, t)
                sl = slice(k * E, (k + 1) * E)
                three(YB[:], W_hi[:, 2, sl], W_lo[:, 2, sl], h_hi[:, k % NH], h_lo[:, k % NH],
                      k == 0, k == K - 1).then_inc(Y_done, 1)

            def macro(t, u):
                for k in range(K):
                    if has(t) and k + LEAD < K:
                        up(t, u, k + LEAD)
                    if has(t + 1) and k + LEAD >= K:
                        up(t + 1, 1 - u, k + LEAD - K)
                    if k == 0 and has(t + 1):
                        turn_x2(t + 1)
                    if k == 1 and has(t - 1):
                        turn_y(t - 1)
                    if k == 3 and has(t + 2):
                        turn_global_probs(t + 2)
                    if k == 3 and has(t + 1):
                        score_experts(t + 1, 1 - u)
                    if k == 5 and has(t + 2):
                        window_context(t + 2)
                    if k == 5 and has(t + 3):
                        turn_x1(t + 3, 1 - u)
                    if k == 4 and has(t + 2):
                        mix_global(t + 2, u)
                    if k == 6 and has(t + 3):
                        project_qk(t + 3)
                    if k == 7 and has(t + 3):
                        project_v(t + 3)
                    if k == 7 and has(t + 2):
                        project_mix(t + 2)
                    if k == 9 and has(t + 3):
                        fold_keys(t + 3)
                    if k == 9 and has(t + 1):
                        turn_weights(t + 1)
                    if k == 9 and has(t + 2):
                        project_out(t + 2)
                    if k == 11 and has(t + 3):
                        score_windows(t + 3)
                    if k == 12 and has(t + 3):
                        score_global(t + 3)
                    if has(t):
                        down(t, k)

            pe.wait_ge(ident_ready, 1)
            pe.wait_ge(small_in, 9 * 16)
            nc.tensor.transpose(P0[:, 0:P], Wk[:], ident[:]).then_inc(wkT_done, 1)
            pe.wait_ge(wkT_ready, 1)
            over_tiles(pe, macro)
            turn_y(NT - 1)


_INS = ['L0_attn_hidden_states', 'L0_attn_Wq', 'L0_attn_bq', 'L0_attn_Wk', 'L0_attn_bk', 'L0_attn_Wv', 'L0_attn_bv',
        'L0_attn_Wo', 'L0_attn_bo', 'L0_ffn_gate_kernel', 'L0_ffn_w0_kernel', 'L0_ffn_w1_kernel', 'L0_ffn_wo_kernel']


def kernel(**inputs):
    import numpy as _np
    import concourse.bacc as _bacc
    from concourse import mybir as _mybir
    from concourse.bass_utils import run_bass_kernel_spmd as _run

    nc = _bacc.Bacc("TRN2", target_bir_lowering=False, num_devices=1)
    arrays, args = {}, []
    for name in _INS:
        a = _np.ascontiguousarray(inputs[name])
        arrays[f"in_{name}_dram"] = a
        args.append(nc.dram_tensor(f"in_{name}_dram", a.shape, _mybir.dt.from_np(a.dtype), kind="ExternalInput").ap())
    shape = tuple(inputs['L0_attn_hidden_states'].shape)
    args.append(nc.dram_tensor("out_0_dram", shape, _mybir.dt.float32, kind="ExternalOutput").ap())
    preln_attention_moe_kernel(nc, *args)
    r = _run(nc, [arrays], core_ids=[0])
    return r.results[0]["out_0_dram"]
```

```python
import concourse.bass as bass
from concourse import mybir
from contextlib import ExitStack


def preln_attention_moe_kernel(
    nc: bass.Bass,
    x: bass.AP,
    wq: bass.AP,
    bq: bass.AP,
    wk: bass.AP,
    bk: bass.AP,
    wv: bass.AP,
    bv: bass.AP,
    wo: bass.AP,
    bo: bass.AP,
    gate: bass.AP,
    w0: bass.AP,
    w1: bass.AP,
    w2: bass.AP,
    out: bass.AP,
):
    fp32 = mybir.dt.float32
    fp32r = mybir.dt.float32r
    u32 = mybir.dt.uint32
    ALU = mybir.AluOpType
    ACT = mybir.ActivationFunctionType
    AX = mybir.AxisListType

    NSEQ, SEQ, E = x.shape
    NE, _, H = w0.shape
    HEADS, D, WIN = 16, 8, 32
    SCALE = float(D) ** -0.5
    EPS = 1e-5
    P = 128
    NB = 4
    TOK = NB * P
    NT = NSEQ * SEQ // TOK
    NS = TOK // SEQ
    HC = H // P
    K = NE * HC
    LEAD = 4
    LAG = 2
    HG = HEADS // 4
    QC = WIN + 1
    GR = 32
    NH = 4
    EARLY = 2
    NQ = 4
    NW = 3 * NE
    NV = NW * 2 // 3

    x_v = x.rearrange("s l e -> (s l) e").rearrange("(t j p) e -> t p j e", j=NB, p=P)
    out_v = out.rearrange("s l e -> (s l) e").rearrange("(t j p) e -> t p j e", j=NB, p=P)
    w_rows = nc.dram_tensor("routing_rows", (NT, NE * TOK), fp32).ap()

    ctx = ExitStack()
    with ctx:
        def sb(name, shape, dt=fp32):
            return ctx.enter_context(nc.sbuf_tensor(name, shape, dt))

        def pb(name, shape, dt=fp32):
            return ctx.enter_context(nc.psum_tensor(name, shape, dt))

        def sem(name):
            return ctx.enter_context(nc.semaphore(name))

        ident = sb("ident", [P, P])
        head_mask = sb("head_mask", [P, GR])
        group_rows = sb("group_rows", [P, HG])
        in_group = sb("in_group", [P, 4])
        expert_no = sb("expert_no", [P, NE])
        half_power = sb("half_power", [P, NB])
        eps = sb("eps", [P, NB])
        idle = sb("idle", [P, 5])
        Wq, Wk, Wv, Wo, WkT = (sb(n, [P, E]) for n in ("Wq", "Wk", "Wv", "Wo", "WkT"))
        Bq, Bk, Bv = (sb(n, [P, 1]) for n in ("Bq", "Bk", "Bv"))
        Bo = sb("Bo", [P, E])
        G_in = sb("G_in", [P, NE])
        G_parts = sb("G_parts", [P, 2 * NE], fp32r)
        W2_in = sb("W2_in", [P, NE * H])
        W_hi, W_lo = sb("W_hi", [P, 3, NE * H], fp32r), sb("W_lo", [P, 3, NE * H], fp32r)

        X = sb("X", [P, NT * TOK])

        stats1, stats2 = sb("stats1", [P, NB, 6]), sb("stats2", [P, NB, 6])
        mv1, mv2 = sb("mv1", [P, NB, 2]), sb("mv2", [P, NB, 2])
        var1, var2 = sb("var1", [P, NB]), sb("var2", [P, NB])
        rstd1, rstd2 = sb("rstd1", [P, NB]), sb("rstd2", [P, NB])
        mr1, mr2 = sb("mr1", [P, NB]), sb("mr2", [P, NB])
        shift1, shift2 = sb("shift1", [P, NB]), sb("shift2", [P, NB])
        xn1, xn2 = sb("xn1", [P, 2, NB, E]), sb("xn2", [P, NB, E])
        xT = sb("xT", [P, TOK])
        xT_win = sb("xT_win", [P, NB * WIN])
        QT, KT = sb("QT", [P, NB, QC]), sb("KT", [P, NB, WIN])
        q_glob = sb("q_glob", [P, NS, GR])
        q_heads = sb("q_heads", [P, NB, 4, WIN])
        k_groups = sb("k_groups", [P, NB, HG, WIN])
        v_heads = sb("v_heads", [P, NB, E])
        U, c_glob = sb("U", [P, NS * GR]), sb("c_glob", [NS * GR, 1])
        sg, pg = sb("sg", [NS * GR, SEQ]), sb("pg", [NS * GR, SEQ])
        pgn = sb("pgn", [NS * GR, SEQ])
        gmax, gshift, gsum, grec = (sb(n, [NS * GR, 1]) for n in ("gmax", "gshift", "gsum", "grec"))
        pgT = sb("pgT", [P, 2, NS * GR])
        gmix = sb("gmix", [P, NS * GR])
        zmask, zctx = sb("zmask", [P, NS, GR]), sb("zctx", [P, NS])
        wmax, wsum, wrec = (sb(n, [P, HG * NB]) for n in ("wmax", "wsum", "wrec"))
        ws, wp, wpn, wpT = (sb(n, [P, TOK]) for n in ("ws", "wp", "wpn", "wpT"))
        C = sb("C", [P, NB, QC])

        lg_parts = sb("lg_parts", [P, NB, 2, NE])
        lg, top = sb("lg", [P, NB, NE]), sb("top", [P, NB, 8])
        top_no, top_nof = sb("top_no", [P, NB, 8], u32), sb("top_nof", [P, NB, 2])
        gap, tanh_gap = sb("gap", [P, NB]), sb("tanh_gap", [P, NB])
        share = sb("share", [P, 2, NB])
        pick = sb("pick", [P, 2, NE, NB])
        picked = sb("picked", [P, 2, NE, NB])
        W_tok = sb("W_tok", [P, NE, NB])
        w_tile = sb("w_tile", [NE * NB, P])

        Wb = sb("Wb", [P, 2, NE * TOK])
        W_in = [Wb[:, 1, 0:NE * H], Wb[:, 1, NE * H:2 * NE * H], W2_in[:]]
        x_hi, x_lo = sb("x_hi", [P, 2, TOK], fp32r), sb("x_lo", [P, 2, TOK], fp32r)
        sil, hid = sb("sil", [P, 2, TOK]), sb("hid", [P, NH, TOK])
        h_hi, h_lo = sb("h_hi", [P, NH, TOK], fp32r), sb("h_lo", [P, NH, TOK], fp32r)
        yT = sb("yT", [P, TOK])
        y_out = sb("y_out", [P, 2, NB, E])

        AB = pb("AB", [P, 2, 2, TOK])
        YB = pb("YB", [P, TOK])
        P0, P1, P2 = pb("P0", [P, TOK]), pb("P1", [P, TOK]), pb("P2", [P, TOK])

        x_in = [sem("x_in0"), sem("x_in1")]
        small_in, moe_in = sem("small_in"), sem("moe_in")
        consts_ready, ident_ready, wkT_done, wkT_ready = (
            sem(n) for n in ("consts_ready", "ident_ready", "wkT_done", "wkT_ready"))
        w_hi_ready, w_lo_ready, w_lo_pool_ready = (
            sem(n) for n in ("w_hi_ready", "w_lo_ready", "w_lo_pool_ready"))
        (stats1_ready, scale1_ready, xn1_ready, T1_done, xT_ready, QK_done, QT_ready, KT_ready,
         q_glob_ready, qk_spread, U_done, U_ready, V_done, v_heads_ready, G_done, sg_ready,
         pg_ready, pgn_ready, S_done, ws_ready, wp_ready, wrec_ready, wpn_ready, wpT_ready,
         pgT_ready, mix_done, gmix_ready, Z_done, zctx_ready, CT_done, C_ready,
         O_done, bo_added, x1_ready, stats2_ready, scale2_ready, xn2_ready, T2_done, x_hi_ready,
         x_lo_ready, logits_done, lg_ready, gap_ready, tanh_ready, share_ready, W_tok_ready,
         w_tile_ready) = (
            sem(n) for n in (
                "stats1_ready", "scale1_ready", "xn1_ready", "T1_done", "xT_ready", "QK_done",
                "QT_ready", "KT_ready", "q_glob_ready", "qk_spread", "U_done", "U_ready",
                "V_done", "v_heads_ready", "G_done", "sg_ready", "pg_ready", "pgn_ready",
                "S_done", "ws_ready", "wp_ready", "wrec_ready", "wpn_ready", "wpT_ready",
                "pgT_ready", "mix_done", "gmix_ready", "Z_done", "zctx_ready",
                "CT_done", "C_ready", "O_done", "bo_added", "x1_ready", "stats2_ready",
                "scale2_ready", "xn2_ready", "T2_done", "x_hi_ready", "x_lo_ready",
                "logits_done", "lg_ready", "gap_ready", "tanh_ready", "share_ready",
                "W_tok_ready", "w_tile_ready"))
        rows_out = sem("rows_out")
        wb_in = [sem(f"wb_in{q}") for q in range(NQ)]
        A_done, B_done, sil_ready, prod_ready, hid_ready, h_hi_ready, h_lo_ready, Y_done = (
            sem(n) for n in ("A_done", "B_done", "sil_ready", "prod_ready", "hid_ready",
                             "h_hi_ready", "h_lo_ready", "Y_done"))
        yT_ready, OT_done, y_kept, y_ready = (sem(n) for n in ("yT_ready", "OT_done", "y_kept", "y_ready"))
        stored = [sem("stored0"), sem("stored1")]

        def need(eng, s, n):
            if not (isinstance(n, int) and n <= 0):
                eng.wait_ge(s, n)

        def tile_of(a, rows=P):
            return X[0:rows, bass.ds(a * TOK, TOK)]

        def has(a):
            return not isinstance(a, int) or 0 <= a < NT

        def most(a):
            return min(a, NT) if isinstance(a, int) else a

        def has_product(t, k):
            return has(t) and not (isinstance(t, int) and t == 0 and k < EARLY)

        def has_front(t):
            return has(t + 3) and not (isinstance(t, int) and t == 0)

        def over_tiles(eng, opening, macro):
            for t in range(-3, 0):
                opening(t, t % 2)
            macro(0, 0)
            with eng.Fori(0, (NT - 4) // 2, 1) as i:
                macro(i * 2 + 1, 1)
                macro(i * 2 + 2, 0)
            for t in range(NT - 3, NT):
                macro(t, t % 2)

        block = ctx.enter_context(nc.Block())

        @block.sync
        def _(sp):
            def load_x(a, u):
                need(sp, x_in[u], (a - u) // 2 * 16 if isinstance(a, int) else (a - u) * 8)
                sp.dma_start(tile_of(a).rearrange("p (j e) -> p j e", j=NB),
                             x_v[bass.ds(a, 1)].rearrange("a p j e -> (a p) j e")
                             if not isinstance(a, int) else x_v[a]).then_inc(x_in[u], 16)

            load_x(0, 0)
            for dst, src in ((Wq, wq), (Wk, wk), (Wv, wv), (Wo, wo), (G_in, gate)):
                sp.dma_start(dst[:], src).then_inc(small_in, 16)
            for dst, src in ((Bq, bq), (Bk, bk), (Bv, bv)):
                sp.dma_start(dst[:], src.rearrange("(p o) -> p o", o=1)).then_inc(small_in, 16)
            sp.dma_start(Bo[:], bo.rearrange("(o e) -> o e", o=1).broadcast_to([P, E])).then_inc(small_in, 16)
            load_x(1, 1)
            with sp.Fori(1, NT // 2, 1) as i:
                load_x(i * 2, 0)
                load_x(i * 2 + 1, 1)

            def spread_routing(a, u):
                if isinstance(a, int) and a == 1:
                    sp.wait_ge(w_lo_ready, NV + 1)
                    sp.wait_ge(w_lo_pool_ready, NW - NV)
                sp.wait_ge(w_tile_ready, a + 1)
                sp.dma_start(w_rows[bass.ds(a, 1)].rearrange("o (r p) -> (o r) p", p=P), w_tile[:]).then_inc(rows_out, 16)
                sp.wait_ge(rows_out, a * 16 + 16)
                part = NE * TOK // NQ
                for q in range(NQ):
                    sp.dma_start(Wb[:, u, q * part:(q + 1) * part],
                                 w_rows[bass.ds(a, 1), q * part:(q + 1) * part].broadcast_to([P, part])).then_inc(wb_in[q], 16)

            def store(t, u):
                sp.wait_ge(y_ready, t + 1)
                dst = out_v[t] if isinstance(t, int) else out_v[bass.ds(t, 1)].rearrange("a p j e -> (a p) j e")
                sp.dma_start(dst, y_out[:, u]).then_inc(stored[u], 16)

            def macro(t, u):
                if has(t - 1):
                    store(t - 1, 1 - u)
                if has(t + 1):
                    spread_routing(t + 1, 1 - u)

            def opening(t, u):
                if has(t + 1):
                    spread_routing(t + 1, 1 - u)

            over_tiles(sp, opening, macro)
            store(NT - 1, (NT - 1) % 2)
            for u in range(2):
                sp.wait_ge(stored[u], NT // 2 * 16)

        @block.gpsimd
        def _(pool):
            g = nc.gpsimd
            g.memset(ident[:], 0.0)
            g.memset(head_mask[:], 1.0)
            g.memset(v_heads[:], 0.0)
            g.memset(half_power[:], -0.5)
            g.memset(eps[:], EPS)
            g.memset(C[:], 0.0)
            for n in range(NE):
                g.memset(expert_no[:, n:n + 1], float(n))
            pool.drain()
            g.affine_select(out=ident[:], in_=ident[:], compare_op=ALU.not_equal, fill=1.0, base=0,
                            pattern=[[-1, P]], channel_multiplier=1).then_inc(ident_ready, 1)
            g.affine_select(out=head_mask[:], in_=head_mask[:], compare_op=ALU.is_ge, fill=0.0, base=0,
                            pattern=[[-D, GR]], channel_multiplier=1)
            pool.drain()
            g.affine_select(out=head_mask[:], in_=head_mask[:], compare_op=ALU.is_ge, fill=0.0, base=D - 1,
                            pattern=[[D, GR]], channel_multiplier=-1).then_inc(consts_ready, 1)
            pool.drain()
            g.tensor_tensor(in_group[:], head_mask[:, 0:4], head_mask[:, 4:8], ALU.add)
            pool.drain()
            g.tensor_tensor(in_group[:], in_group[:], head_mask[:, 8:12], ALU.add)
            pool.drain()
            g.tensor_tensor(in_group[:], in_group[:], head_mask[:, 12:16], ALU.add)
            g.memset(group_rows[:], 1.0)
            pool.drain()
            g.affine_select(out=group_rows[:], in_=group_rows[:], compare_op=ALU.is_ge, fill=0.0, base=0,
                            pattern=[[-4 * D, HG]], channel_multiplier=1)
            pool.drain()
            g.affine_select(out=group_rows[:], in_=group_rows[:], compare_op=ALU.is_ge, fill=0.0, base=4 * D - 1,
                            pattern=[[4 * D, HG]], channel_multiplier=-1)
            pool.drain()

            def norm_scale(a, stats_ready, mv, var, rstd, mr, shift, used, ready):
                pool.wait_ge(stats_ready, a + 1)
                need(pool, used, a)
                g.tensor_tensor(var[:], mv[:, :, 1], eps[:], ALU.add)
                pool.drain()
                g.tensor_tensor(rstd[:], var[:], half_power[:], ALU.pow)
                pool.drain()
                g.tensor_tensor(mr[:], mv[:, :, 0], rstd[:], ALU.mult)
                pool.drain()
                g.tensor_scalar(shift[:], mr[:], -1.0, None, ALU.mult).then_inc(ready, 1)

            def scale1(a):
                norm_scale(a, stats1_ready, mv1, var1, rstd1, mr1, shift1, xn1_ready, scale1_ready)

            def scale2(a):
                norm_scale(a, stats2_ready, mv2, var2, rstd2, mr2, shift2, xn2_ready, scale2_ready)

            def spread_q_glob(a):
                pool.wait_ge(QT_ready, a + 1)
                need(pool, U_done, a)
                g.tensor_tensor(q_glob[:], QT[:, 0:NB:2, 0:1].broadcast_to([P, NS, GR]),
                                head_mask[:].unsqueeze(1).broadcast_to([P, NS, GR]), ALU.mult).then_inc(q_glob_ready, 1)

            def spread_q(a):
                need(pool, S_done, a)
                g.tensor_tensor(q_heads[:], QT[:, :, 1:QC].unsqueeze(2).broadcast_to([P, NB, 4, WIN]),
                                in_group[:].unsqueeze(1).unsqueeze(3).broadcast_to([P, NB, 4, WIN]), ALU.mult)

            def spread_k(a):
                pool.wait_ge(KT_ready, a + 1)
                g.tensor_tensor(k_groups[:], KT[:].unsqueeze(2).broadcast_to([P, NB, HG, WIN]),
                                group_rows[:].unsqueeze(1).unsqueeze(3).broadcast_to([P, NB, HG, WIN]),
                                ALU.mult).then_inc(qk_spread, 1)

            def add_bo(a):
                pool.wait_ge(xn1_ready, a + 1)
                xt = tile_of(a).rearrange("p (j e) -> p j e", j=NB)
                g.tensor_tensor(xt, xt, Bo[:].unsqueeze(1).broadcast_to([P, NB, E]), ALU.add).then_inc(bo_added, 1)

            def window_probs(a):
                pool.wait_ge(wrec_ready, a + 1)
                need(pool, wpT_ready, a)
                g.tensor_tensor(wpn[:].rearrange("p (b k) -> p b k", k=WIN), wp[:].rearrange("p (b k) -> p b k", k=WIN),
                                wrec[:].unsqueeze(2).broadcast_to([P, HG * NB, WIN]), ALU.mult).then_inc(wpn_ready, 1)

            def token_weights(a):
                pool.wait_ge(share_ready, a + 1)
                need(pool, w_tile_ready, a)
                g.tensor_tensor(picked[:], pick[:], share[:].unsqueeze(2).broadcast_to([P, 2, NE, NB]), ALU.mult)
                pool.drain()
                g.tensor_tensor(W_tok[:], picked[:, 0], picked[:, 1], ALU.add).then_inc(W_tok_ready, 1)

            def weight(t, u, k):
                if k % (K // NQ) == 0:
                    pool.wait_ge(wb_in[k // (K // NQ)], t * 16 + 16)
                pool.wait_ge(prod_ready, t * K + k + 1)
                n = k // HC
                h = hid[:, k % NH]
                g.tensor_tensor(h, h, Wb[:, u, n * TOK:(n + 1) * TOK], ALU.mult).then_inc(hid_ready, 1)

            def finish(t, u):
                pool.wait_ge(y_kept, t + 1)
                out_t = y_out[:, u].rearrange("p j e -> p (j e)")
                g.tensor_tensor(out_t, out_t, tile_of(t), ALU.add).then_inc(y_ready, 1)

            def macro(t, u):
                for k in range(K):
                    if has(t):
                        weight(t, u, k)
                    if k == 5 and has_front(t):
                        scale1(t + 3)
                    if k == 4 and has(t + 2):
                        window_probs(t + 2)
                    if k == 6 and has(t - 1):
                        finish(t - 1, 1 - u)
                    if k == 8 and has(t + 2):
                        add_bo(t + 2)
                    if k == 11 and has(t + 3):
                        spread_q_glob(t + 3)
                    if k == 11 and has(t + 1):
                        token_weights(t + 1)
                    if k == 12 and has(t + 3):
                        spread_q(t + 3)
                    if k == 13 and has(t + 3):
                        spread_k(t + 3)
                    if k == 14 and has(t + 2):
                        scale2(t + 2)

            def opening(t, u):
                spread_q_glob(t + 3)
                if has(t + 2):
                    window_probs(t + 2)
                spread_q(t + 3)
                spread_k(t + 3)
                if has(t + 1):
                    token_weights(t + 1)
                if has(t + 2):
                    add_bo(t + 2)
                scale1(t + 4)
                if t == -2:
                    rest_weights(range(NV, NW))
                if has(t + 2):
                    scale2(t + 2)

            def rest_weights(parts):
                for i in parts:
                    m, sl = i // NE, slice(i % NE * H, (i % NE + 1) * H)
                    pool.wait_ge(w_hi_ready, i + 2)
                    g.tensor_tensor(W_lo[:, m, sl], W_in[m][:, sl], W_hi[:, m, sl], ALU.subtract).then_inc(w_lo_pool_ready, 1)

            scale1(0)
            pool.wait_ge(small_in, 9 * 16)
            over_tiles(pool, opening, macro)
            finish(NT - 1, (NT - 1) % 2)

        @block.scalar
        def _(act):
            s = nc.scalar

            def normalise1(a, u, j):
                if j == 0:
                    act.wait_ge(scale1_ready, a + 1)
                    need(act, mix_done, a - 1)
                    s.activation(idle[:, 0:1], rstd1[:, 0:1], ACT.Copy)
                ins = s.activation(xn1[:, u, j], X[:, bass.ds(a * TOK + j * E, E)], ACT.Identity,
                                   scale=rstd1[:, j:j + 1], bias=shift1[:, j:j + 1])
                if j == NB - 1:
                    ins.then_inc(xn1_ready, 1)

            def keep_xT(a):
                act.wait_ge(T1_done, a + 1)
                need(act, G_done, a)
                s.activation(xT[:], P0[:], ACT.Identity)
                win = P0[:].rearrange("p (j q) -> p j q", q=P)[:, :, 1:QC]
                s.activation(xT_win[:].rearrange("p (j k) -> p j k", k=WIN), win, ACT.Identity).then_inc(xT_ready, 1)

            def keep_qk(a):
                act.wait_ge(QK_done, a + 1)
                need(act, qk_spread, a)
                nq = NB * QC
                s.activation(QT[:], P0[:, 0:nq].rearrange("p (j q) -> p j q", q=QC), ACT.Identity,
                             bias=Bq[:, 0:1]).then_inc(QT_ready, 1)
                s.activation(KT[:], P0[:, nq:nq + NB * WIN].rearrange("p (j q) -> p j q", q=WIN), ACT.Identity,
                             bias=Bk[:, 0:1]).then_inc(KT_ready, 1)

            def keep_U(a):
                act.wait_ge(U_done, a + 1)
                need(act, sg_ready, a)
                s.activation(c_glob[:], P1[0:NS * GR, NS * GR:NS * GR + 1], ACT.Identity)
                s.activation(U[:], P1[:, 0:NS * GR], ACT.Identity).then_inc(U_ready, 1)

            def exps(a):
                act.wait_ge(sg_ready, a + 1)
                need(act, pgn_ready, a)
                s.activation(pg[:], sg[:], ACT.Exp, scale=SCALE, bias=gshift[:, 0:1],
                             accum_out=gsum[:, 0:1]).then_inc(pg_ready, 1)
                act.wait_ge(ws_ready, a + 1)
                need(act, wpn_ready, a)
                s.activation(wp[:], ws[:], ACT.Exp, scale=SCALE).then_inc(wp_ready, 1)

            def keep_context(a):
                act.wait_ge(CT_done, a + 1)
                need(act, O_done, a)
                s.activation(C[:, :, 1:QC], P1[:, 0:NB * WIN].rearrange("p (j q) -> p j q", q=WIN), ACT.Identity,
                             bias=Bv[:, 0:1]).then_inc(C_ready, 1)

            def split_x(a, u):
                act.wait_ge(T2_done, a + 1)
                need(act, B_done, a * K - K)
                s.activation(x_hi[:, u], P0[:], ACT.Copy).then_inc(x_hi_ready, 1)

            def keep_logits(a):
                act.wait_ge(logits_done, a + 1)
                need(act, share_ready, a)
                s.activation(lg_parts[:], P0[:, 0:2 * NB * NE].rearrange("p (j r n) -> p j r n", r=2, n=NE), ACT.Copy).then_inc(lg_ready, 1)

            def tanh(a):
                act.wait_ge(gap_ready, a + 1)
                s.activation(tanh_gap[:], gap[:], ACT.Tanh, scale=0.5).then_inc(tanh_ready, 1)

            def silu(t, k):
                act.wait_ge(A_done, t * K + k + 1)
                need(act, prod_ready, t * K + k - 1)
                s.activation(sil[:, k % 2], AB[:, k % 2, 0], ACT.Silu).then_inc(sil_ready, 1)

            def split_h(t, k):
                act.wait_ge(hid_ready, t * K + k + 1)
                need(act, Y_done, t * K + k - NH + 1)
                s.activation(h_hi[:, k % NH], hid[:, k % NH], ACT.Copy).then_inc(h_hi_ready, 1)

            def split_weights(parts):
                act.wait_ge(moe_in, 3 * 16)
                for i in parts:
                    m, sl = i // NE, slice(i % NE * H, (i % NE + 1) * H)
                    s.activation(W_hi[:, m, sl], W_in[m][:, sl], ACT.Copy).then_inc(w_hi_ready, 1)

            def keep_experts(t, u):
                act.wait_ge(OT_done, t + 1)
                need(act, stored[u], (t - u) // 2 * 16 if isinstance(t, int) else (t - u) * 8)
                s.activation(y_out[:, u].rearrange("p j e -> p (j e)"), P1[:], ACT.Copy).then_inc(y_kept, 1)

            def macro(t, u):
                for k in range(K):
                    if has_product(t, k):
                        silu(t, k)
                    if k == 3 and has(t + 2):
                        exps(t + 2)
                    if k >= LAG and has(t):
                        split_h(t, k - LAG)
                    if k < LAG and has(t - 1):
                        split_h(t - 1, K + k - LAG)
                    if k == 5 and has(t - 1):
                        keep_experts(t - 1, 1 - u)
                    if k in (7, 8) and has_front(t):
                        for j in range(2 * (k - 7), 2 * (k - 6)):
                            normalise1(t + 3, 1 - u, j)
                    if k == 4 and has(t + 1):
                        split_x(t + 1, 1 - u)
                    if k == 8 and has(t + 1):
                        keep_logits(t + 1)
                    if k == 10 and has(t + 2):
                        keep_context(t + 2)
                    if k == 9 and has_front(t):
                        keep_xT(t + 3)
                    if k == 11 and has(t + 3):
                        keep_qk(t + 3)
                    if k == 10 and has(t + 1):
                        tanh(t + 1)
                    if k == 14 and has(t + 3):
                        keep_U(t + 3)

            def opening(t, u):
                if t == -2:
                    exps(t + 2)
                keep_qk(t + 3)
                if t == -2:
                    split_weights(range(0, NW * 3 // 4))
                if t == -1:
                    split_x(t + 1, 1 - u)
                    exps(t + 2)
                if has(t + 1):
                    keep_logits(t + 1)
                    tanh(t + 1)
                if has(t + 2):
                    keep_context(t + 2)
                if has(t + 1):
                    silu(t + 1, 0)
                if t == -3:
                    keep_U(t + 3)
                for j in range(NB):
                    normalise1(t + 4, u, j)
                if t == -2:
                    split_weights(range(NW * 3 // 4, NW))
                if t > -3:
                    keep_U(t + 3)
                if has(t + 1):
                    silu(t + 1, 1)
                keep_xT(t + 4)

            for j in range(NB):
                normalise1(0, 0, j)
            act.wait_ge(small_in, 9 * 16)
            act.dma_start(W_in[0].rearrange("p (n h) -> p n h", n=NE), w0.rearrange("n e h -> e n h")).then_inc(moe_in, 16)
            act.dma_start(W_in[1].rearrange("p (n h) -> p n h", n=NE), w1.rearrange("n e h -> e n h")).then_inc(moe_in, 16)
            act.dma_start(W_in[2].rearrange("p (n e) -> p n e", e=E), w2.rearrange("n (c p) e -> p (n c) e", p=P)).then_inc(moe_in, 16)
            keep_xT(0)
            act.wait_ge(wkT_done, 1)
            s.activation(WkT[:], YB[:, 0:P], ACT.Identity).then_inc(wkT_ready, 1)
            s.activation(G_parts[:, 0:NE], G_in[:], ACT.Copy).then_inc(w_hi_ready, 1)
            act.wait_ge(consts_ready, 1)
            over_tiles(act, opening, macro)
            for k in range(K - LAG, K):
                split_h(NT - 1, k)
            keep_experts(NT - 1, (NT - 1) % 2)

        @block.vector
        def _(dve):
            v = nc.vector

            def statistics(a, stats, mv, used, ready, spare):
                need(dve, used, a)
                v.memset(idle[:, spare:spare + 1], 0.0)
                for j in range(NB):
                    v.bn_stats(stats[:, j], X[:, bass.ds(a * TOK + j * E, E)])
                dve.drain()
                for j in range(NB):
                    last = v.bn_aggr(mv[:, j], stats[:, j])
                last.then_inc(ready, 1)

            def statistics1(a, u):
                dve.wait_ge(x_in[u], (a - u) // 2 * 16 + 16 if isinstance(a, int) else (a - u) * 8 + 16)
                statistics(a, stats1, mv1, scale1_ready, stats1_ready, 2)

            def statistics2(a):
                dve.wait_ge(x1_ready, a + 1)
                statistics(a, stats2, mv2, scale2_ready, stats2_ready, 3)

            def normalise2(a):
                dve.wait_ge(scale2_ready, a + 1)
                need(dve, T2_done, a)
                v.memset(idle[:, 1:2], 0.0)
                for j in range(NB):
                    last = v.tensor_scalar(xn2[:, j], X[:, bass.ds(a * TOK + j * E, E)],
                                           rstd2[:, j:j + 1], shift2[:, j:j + 1], ALU.mult, ALU.add)
                last.then_inc(xn2_ready, 1)

            def spread_v(a):
                dve.wait_ge(V_done, a + 1)
                need(dve, CT_done, a)
                for w in range(NB):
                    for h in range(4):
                        src = P1[w * WIN:(w + 1) * WIN, 0:E].rearrange("p (c g d) -> p c g d", g=4, d=D)[:, :, h]
                        dst = v_heads[h * WIN:(h + 1) * WIN, w].rearrange("p (c g d) -> p c g d", g=4, d=D)[:, :, h]
                        last = v.tensor_copy(dst, src)
                last.then_inc(v_heads_ready, 1)

            def global_scores(a):
                dve.wait_ge(G_done, a + 1)
                dve.wait_ge(U_ready, a + 1)
                need(dve, pg_ready, a)
                v.tensor_scalar(sg[:], P2[0:NS * GR, 0:SEQ], c_glob[:, 0:1], None, ALU.add)
                dve.drain()
                v.tensor_reduce(gmax[:], sg[:], AX.X, ALU.max)
                dve.drain()
                v.tensor_scalar(gshift[:], gmax[:], -SCALE, None, ALU.mult).then_inc(sg_ready, 1)

            def window_scores(a):
                dve.wait_ge(S_done, a + 1)
                need(dve, wp_ready, a)
                sc = P1[:].rearrange("p (b k) -> p b k", k=WIN)
                v.tensor_reduce(wmax[:], sc, AX.X, ALU.max)
                dve.drain()
                v.tensor_tensor(ws[:].rearrange("p (b k) -> p b k", k=WIN), sc,
                                wmax[:].unsqueeze(2).broadcast_to([P, HG * NB, WIN]), ALU.subtract).then_inc(ws_ready, 1)

            def global_probs(a):
                dve.wait_ge(pg_ready, a + 1)
                need(dve, pgT_ready, a)
                v.reciprocal(grec[:], gsum[:])
                dve.drain()
                v.tensor_scalar(pgn[:], pg[:], grec[:, 0:1], None, ALU.mult).then_inc(pgn_ready, 1)

            def window_sums(a):
                dve.wait_ge(wp_ready, a + 1)
                need(dve, wpn_ready, a)
                v.tensor_reduce(wsum[:], wp[:].rearrange("p (b k) -> p b k", k=WIN), AX.X, ALU.add)
                dve.drain()
                v.reciprocal(wrec[:], wsum[:]).then_inc(wrec_ready, 1)

            def turn_probs(a):
                dve.wait_ge(wpn_ready, a + 1)
                need(dve, CT_done, a)
                v.transpose(wpT[:], wpn[:]).then_inc(wpT_ready, 1)

            def turn_global_probs(a):
                dve.drain()
                need(dve, mix_done, a)
                for b in range(NS):
                    for q in range(P // GR):
                        rows = slice(b * GR, (b + 1) * GR)
                        src = pgn[rows].rearrange("r (c q k) -> r c q k", c=SEQ // P, k=GR)[:, :, q]
                        last = v.transpose(pgT[q * GR:(q + 1) * GR, :, rows], src)
                last.then_inc(pgT_ready, 1)

            def keep_mix(a):
                dve.wait_ge(mix_done, a + 1)
                need(dve, Z_done, a)
                v.tensor_copy(gmix[:], P2[:, 0:NS * GR]).then_inc(gmix_ready, 1)

            def global_context(a):
                dve.wait_ge(Z_done, a + 1)
                need(dve, O_done, a)
                v.tensor_tensor(zmask[:], P2[:, 0:NS * GR].rearrange("p (s h) -> p s h", s=NS),
                                head_mask[:].unsqueeze(1).broadcast_to([P, NS, GR]), ALU.mult)
                dve.drain()
                v.tensor_reduce(zctx[:], zmask[:], AX.X, ALU.add)
                dve.drain()
                v.tensor_scalar(C[:, 0:NB:2, 0], zctx[:], Bv[:, 0:1], None, ALU.add).then_inc(zctx_ready, 1)

            def add_attention(a):
                dve.wait_ge(O_done, a + 1)
                dve.wait_ge(bo_added, a + 1)
                xt = tile_of(a, QC)
                v.tensor_tensor(xt, xt, P0[0:QC, :], ALU.add).then_inc(x1_ready, 1)

            def rest_x(a, u):
                dve.wait_ge(x_hi_ready, a + 1)
                need(dve, B_done, a * K - K)
                v.tensor_tensor(x_lo[:, u], P0[:], x_hi[:, u], ALU.subtract).then_inc(x_lo_ready, 1)

            def top_two(a):
                dve.wait_ge(lg_ready, a + 1)
                need(dve, W_tok_ready, a)
                v.tensor_tensor(lg[:], lg_parts[:, :, 0], lg_parts[:, :, 1], ALU.add)
                dve.drain()
                for j in range(NB):
                    v.max(top[:, j], lg[:, j])
                dve.drain()
                v.tensor_tensor(gap[:], top[:, :, 0], top[:, :, 1], ALU.subtract).then_inc(gap_ready, 1)
                for j in range(NB):
                    v.max_index(top_no[:, j], top[:, j], lg[:, j])
                dve.drain()
                v.tensor_copy(top_nof[:], top_no[:, :, 0:2])
                dve.drain()
                for r in range(2):
                    v.tensor_tensor(pick[:, r], expert_no[:].unsqueeze(2).broadcast_to([P, NE, NB]),
                                    top_nof[:, :, r].unsqueeze(1).broadcast_to([P, NE, NB]), ALU.is_equal)

            def shares(a):
                dve.wait_ge(tanh_ready, a + 1)
                v.tensor_scalar(share[:, 0], tanh_gap[:], 0.5, 0.5, ALU.mult, ALU.add)
                v.tensor_scalar(share[:, 1], tanh_gap[:], -0.5, 0.5, ALU.mult, ALU.add).then_inc(share_ready, 1)

            def turn_weights(a):
                dve.wait_ge(W_tok_ready, a + 1)
                need(dve, rows_out, a * 16)
                for q in range(P // (NE * NB)):
                    rows = slice(q * NE * NB, (q + 1) * NE * NB)
                    last = v.transpose(w_tile[:, rows], W_tok[rows].rearrange("p n j -> p (n j)"))
                last.then_inc(w_tile_ready, 1)

            def product(t, k):
                dve.wait_ge(sil_ready, t * K + k + 1)
                dve.wait_ge(B_done, t * K + k + 1)
                need(dve, h_lo_ready, t * K + k - NH + 1)
                v.tensor_tensor(hid[:, k % NH], sil[:, k % 2], AB[:, k % 2, 1], ALU.mult).then_inc(prod_ready, 1)

            def rest_h(t, k):
                dve.wait_ge(h_hi_ready, t * K + k + 1)
                v.tensor_tensor(h_lo[:, k % NH], hid[:, k % NH], h_hi[:, k % NH], ALU.subtract).then_inc(h_lo_ready, 1)

            def keep_y(t):
                dve.wait_ge(Y_done, t * K + K)
                need(dve, OT_done, t)
                v.tensor_copy(yT[:], YB[:]).then_inc(yT_ready, 1)

            def macro(t, u):
                for k in range(K):
                    if has_product(t, k):
                        product(t, k)
                    if has(t) and k >= LAG:
                        rest_h(t, k - LAG)
                    if k < LAG and has(t - 1):
                        rest_h(t - 1, K + k - LAG)
                    if k == 0 and has(t + 1):
                        normalise2(t + 1)
                    if k == 1 and has(t + 2):
                        global_scores(t + 2)
                    if k == 2 and has(t - 1):
                        keep_y(t - 1)
                    if k == 5 and has_front(t):
                        statistics1(t + 3, 1 - u)
                    if k == 3 and has(t + 2):
                        window_sums(t + 2)
                    if k == 6 and has(t + 2):
                        global_probs(t + 2)
                    if k == 4 and has(t + 1):
                        rest_x(t + 1, 1 - u)
                    if k == 6 and has(t + 2):
                        turn_probs(t + 2)
                    if k == 7 and has(t + 2):
                        turn_global_probs(t + 2)
                    if k == 9 and has(t + 1):
                        top_two(t + 1)
                    if k == 9 and has(t + 2):
                        keep_mix(t + 2)
                    if k == 11 and has(t + 1):
                        shares(t + 1)
                    if k == 11 and has(t + 2):
                        global_context(t + 2)
                    if k == 11 and has(t + 3):
                        spread_v(t + 3)
                    if k == 12 and has(t + 1):
                        turn_weights(t + 1)
                    if k == 13 and has(t + 2):
                        add_attention(t + 2)
                    if k == 14 and has(t + 2):
                        statistics2(t + 2)
                    if k == 15 and has(t + 3):
                        window_scores(t + 3)

            def rest_weights(parts):
                for i in parts:
                    m, sl = i // NE, slice(i % NE * H, (i % NE + 1) * H)
                    dve.wait_ge(w_hi_ready, i + 2)
                    v.tensor_tensor(W_lo[:, m, sl], W_in[m][:, sl], W_hi[:, m, sl], ALU.subtract).then_inc(w_lo_ready, 1)

            def opening(t, u):
                if t == -3:
                    dve.wait_ge(w_hi_ready, 1)
                    v.tensor_tensor(G_parts[:, NE:2 * NE], G_in[:], G_parts[:, 0:NE], ALU.subtract).then_inc(w_lo_ready, 1)
                if has(t + 1):
                    normalise2(t + 1)
                if has(t + 2):
                    global_scores(t + 2)
                if has(t + 1):
                    rest_x(t + 1, 1 - u)
                else:
                    statistics1(t + 4, u)
                if has(t + 2):
                    window_sums(t + 2)
                    global_probs(t + 2)
                    if t == -2:
                        rest_weights(range(0, NV // 4))
                    turn_global_probs(t + 2)
                    turn_probs(t + 2)
                    if t == -2:
                        rest_weights(range(NV // 4, NV * 3 // 4))
                if has(t + 1):
                    top_two(t + 1)
                    shares(t + 1)
                if has(t + 2):
                    keep_mix(t + 2)
                if has(t + 1):
                    statistics1(t + 4, u)
                    turn_weights(t + 1)
                if has(t + 2):
                    global_context(t + 2)
                if has(t + 1):
                    rest_weights(range(NV * 3 // 4, NV))
                spread_v(t + 3)
                if has(t + 1):
                    product(t + 1, 0)
                if has(t + 2):
                    add_attention(t + 2)
                    statistics2(t + 2)
                if has(t + 1):
                    product(t + 1, 1)
                window_scores(t + 3)

            dve.wait_ge(consts_ready, 1)
            statistics1(0, 0)
            over_tiles(dve, opening, macro)
            for k in range(K - LAG, K):
                rest_h(NT - 1, k)
            keep_y(NT - 1)

        @block.tensor
        def _(pe):
            mm = nc.tensor.matmul

            def turn_x1(a, u):
                pe.wait_ge(xn1_ready, a + 1)
                if isinstance(a, int) and a <= 3:
                    need(pe, x1_ready, a - 1)
                    need(pe, lg_ready, a - 2)
                else:
                    pe.wait_ge(lg_ready, a - 1)
                for j in range(NB):
                    last = nc.tensor.transpose(P0[:, j * P:(j + 1) * P], xn1[:, u, j], ident[:])
                last.then_inc(T1_done, 1)

            def project_qk(a):
                pe.wait_ge(xT_ready, a + 1)
                if isinstance(a, int) and a == 3:
                    pe.wait_ge(lg_ready, 2)
                xw = xT[:].rearrange("p (j q) -> p j q", q=P)
                nq = NB * QC
                mm(P0[:, 0:nq], Wq[:], xw[:, :, 0:QC], start=True, stop=True)
                mm(P0[:, nq:nq + NB * WIN], Wk[:], xw[:, :, 1:QC], start=True, stop=True).then_inc(QK_done, 1)

            def project_v(a):
                pe.wait_ge(xT_ready, a + 1)
                need(pe, C_ready, a)
                mm(P1[:, 0:E], xT_win[:], Wv[:], start=True, stop=True).then_inc(V_done, 1)

            def fold_keys(a):
                pe.wait_ge(q_glob_ready, a + 1)
                pe.wait_ge(v_heads_ready, a + 1)
                if isinstance(a, int) and a == 0:
                    pe.wait_ge(wkT_ready, 1)
                qg = q_glob[:].rearrange("p s h -> p (s h)")
                mm(P1[:, 0:NS * GR], WkT[:], qg, start=True, stop=True)
                mm(P1[0:NS * GR, NS * GR:NS * GR + 1], qg, Bk[:], start=True, stop=True).then_inc(U_done, 1)

            def score_global(a):
                pe.wait_ge(U_ready, a + 1)
                need(pe, zctx_ready, a)
                for b in range(NS):
                    last = mm(P2[b * GR:(b + 1) * GR, 0:SEQ], U[:, b * GR:(b + 1) * GR],
                              xT[:, b * SEQ:(b + 1) * SEQ], start=True, stop=True)
                last.then_inc(G_done, 1)

            def score_windows(a):
                pe.wait_ge(qk_spread, a + 1)
                pe.wait_ge(U_ready, a + 1)
                for w in range(NB):
                    last = mm(P1[:, w * P:(w + 1) * P], q_heads[:, w].rearrange("p g q -> p (g q)"),
                              k_groups[:, w].rearrange("p c k -> p (c k)"), start=True, stop=True)
                last.then_inc(S_done, 1)

            def mix_global(a, u):
                pe.wait_ge(pgT_ready, a + 1)
                pe.wait_ge(sg_ready, a + 1)
                for b in range(NS):
                    for c in range(SEQ // P):
                        last = mm(P2[:, b * GR:(b + 1) * GR], xn1[:, u, b * 2 + c], pgT[:, c, b * GR:(b + 1) * GR],
                                  start=(c == 0), stop=(c == SEQ // P - 1))
                last.then_inc(mix_done, 1)

            def project_mix(a):
                pe.wait_ge(gmix_ready, a + 1)
                mm(P2[:, 0:NS * GR], Wv[:], gmix[:], start=True, stop=True).then_inc(Z_done, 1)

            def window_context(a):
                pe.wait_ge(wpT_ready, a + 1)
                pe.wait_ge(v_heads_ready, a + 1)
                need(pe, y_kept, a - 2)
                for w in range(NB):
                    for c in range(HG):
                        col = (w * HG + c) * WIN
                        last = mm(P1[32 * c:32 * (c + 1), w * WIN:(w + 1) * WIN], v_heads[:, w, 32 * c:32 * (c + 1)],
                                  wpT[:, col:col + WIN], start=True, stop=True)
                last.then_inc(CT_done, 1)

            def project_out(a):
                pe.wait_ge(C_ready, a + 1)
                pe.wait_ge(zctx_ready, a + 1)
                pe.wait_ge(KT_ready, most(a + 2))
                if isinstance(a, int):
                    need(pe, lg_ready, a)
                for j in range(NB):
                    last = mm(P0[0:QC, j * E:(j + 1) * E], C[:, j], Wo[:], start=True, stop=True)
                last.then_inc(O_done, 1)

            def turn_x2(a):
                pe.wait_ge(xn2_ready, a + 1)
                if isinstance(a, int) and a <= 1:
                    pe.wait_ge(KT_ready, 3)
                    need(pe, xT_ready, 4 * a)
                for j in range(NB):
                    last = nc.tensor.transpose(P0[:, j * P:(j + 1) * P], xn2[:, j], ident[:])
                last.then_inc(T2_done, 1)

            def score_experts(a, u):
                pe.wait_ge(x_lo_ready, a + 1)
                for j in range(NB):
                    sl = slice(j * P, (j + 1) * P)
                    dst = P0[:, j * 2 * NE:(j + 1) * 2 * NE]
                    mm(dst, x_hi[:, u, sl], G_parts[:], start=True, stop=False)
                    last = mm(dst[:, 0:NE], x_lo[:, u, sl], G_parts[:, 0:NE], start=False, stop=True)
                last.then_inc(logits_done, 1)

            def turn_y(t):
                pe.wait_ge(yT_ready, t + 1)
                pe.wait_ge(ws_ready, most(t + 4))
                if isinstance(t, int):
                    pe.wait_ge(C_ready, most(t + 3))
                    need(pe, y_kept, t)
                for j in range(NB):
                    last = nc.tensor.transpose(P1[:, j * P:(j + 1) * P], yT[:, j * P:(j + 1) * P], ident[:])
                last.then_inc(OT_done, 1)

            def three(dst, w_hi, w_lo, m_hi, m_lo, start, stop):
                mm(dst, w_hi, m_hi, start=start, stop=False)
                mm(dst, w_hi, m_lo, start=False, stop=False)
                return mm(dst, w_lo, m_hi, start=False, stop=stop)

            def up(t, u, k):
                if k == 0:
                    pe.wait_ge(x_lo_ready, t + 1)
                if isinstance(t, int) and t == 0:
                    pe.wait_ge(w_lo_ready, 1 + NE + k // HC + 1)
                need(pe, prod_ready, t * K + k - 1)
                sl = slice(k * P, (k + 1) * P)
                three(AB[:, k % 2, 0], W_hi[:, 0, sl], W_lo[:, 0, sl], x_hi[:, u], x_lo[:, u], True, True).then_inc(A_done, 1)
                three(AB[:, k % 2, 1], W_hi[:, 1, sl], W_lo[:, 1, sl], x_hi[:, u], x_lo[:, u], True, True).then_inc(B_done, 1)

            def down(t, k):
                pe.wait_ge(h_lo_ready, t * K + k + 1)
                if k == 0:
                    need(pe, yT_ready, t)
                    if isinstance(t, int) and t == 0:
                        pe.wait_ge(w_lo_pool_ready, NW - NV)
                sl = slice(k * E, (k + 1) * E)
                three(YB[:], W_hi[:, 2, sl], W_lo[:, 2, sl], h_hi[:, k % NH], h_lo[:, k % NH],
                      k == 0, k == K - 1).then_inc(Y_done, 1)

            def macro(t, u):
                for k in range(K):
                    if has(t) and k + LEAD < K:
                        up(t, u, k + LEAD)
                    if has(t + 1) and k + LEAD >= K:
                        up(t + 1, 1 - u, k + LEAD - K)
                    if k == 0 and has(t + 1):
                        turn_x2(t + 1)
                    if k == 1 and has(t - 1):
                        turn_y(t - 1)
                    if k == 3 and has(t + 1):
                        score_experts(t + 1, 1 - u)
                    if k == 5 and has(t + 2):
                        window_context(t + 2)
                    if k == 5 and has_front(t):
                        turn_x1(t + 3, 1 - u)
                    if k == 5 and has(t + 2):
                        mix_global(t + 2, u)
                    if k == 6 and has(t + 3):
                        project_qk(t + 3)
                    if k == 7 and has(t + 3):
                        project_v(t + 3)
                    if k == 7 and has(t + 2):
                        project_mix(t + 2)
                    if k == 9 and has(t + 3):
                        fold_keys(t + 3)
                    if k == 9 and has(t + 2):
                        project_out(t + 2)
                    if k == 11 and has(t + 3):
                        score_windows(t + 3)
                    if k == 12 and has(t + 3):
                        score_global(t + 3)
                    if has(t):
                        down(t, k)

            def opening(t, u):
                project_qk(t + 3)
                if has(t + 1):
                    turn_x2(t + 1)
                    score_experts(t + 1, 1 - u)
                if has(t + 2):
                    mix_global(t + 2, u)
                    window_context(t + 2)
                if has(t + 2):
                    project_mix(t + 2)
                project_v(t + 3)
                if has(t + 1):
                    up(t + 1, 1 - u, 0)
                if has(t + 2):
                    project_out(t + 2)
                fold_keys(t + 3)
                if has(t + 1):
                    up(t + 1, 1 - u, 1)
                score_windows(t + 3)
                score_global(t + 3)
                turn_x1(t + 4, u)
                if has(t + 1):
                    for k in range(EARLY, LEAD):
                        up(t + 1, 1 - u, k)

            pe.wait_ge(ident_ready, 1)
            turn_x1(0, 0)
            pe.wait_ge(small_in, 9 * 16)
            nc.tensor.transpose(YB[:, 0:P], Wk[:], ident[:]).then_inc(wkT_done, 1)
            over_tiles(pe, opening, macro)
            turn_y(NT - 1)


_INS = ['L0_attn_hidden_states', 'L0_attn_Wq', 'L0_attn_bq', 'L0_attn_Wk', 'L0_attn_bk', 'L0_attn_Wv', 'L0_attn_bv',
        'L0_attn_Wo', 'L0_attn_bo', 'L0_ffn_gate_kernel', 'L0_ffn_w0_kernel', 'L0_ffn_w1_kernel', 'L0_ffn_wo_kernel']


def kernel(**inputs):
    import numpy as _np
    import concourse.bacc as _bacc
    from concourse import mybir as _mybir
    from concourse.bass_utils import run_bass_kernel_spmd as _run

    nc = _bacc.Bacc("TRN2", target_bir_lowering=False, num_devices=1)
    arrays, args = {}, []
    for name in _INS:
        a = _np.ascontiguousarray(inputs[name])
        arrays[f"in_{name}_dram"] = a
        args.append(nc.dram_tensor(f"in_{name}_dram", a.shape, _mybir.dt.from_np(a.dtype), kind="ExternalInput").ap())
    shape = tuple(inputs['L0_attn_hidden_states'].shape)
    args.append(nc.dram_tensor("out_0_dram", shape, _mybir.dt.float32, kind="ExternalOutput").ap())
    preln_attention_moe_kernel(nc, *args)
    r = _run(nc, [arrays], core_ids=[0])
    return r.results[0]["out_0_dram"]
```
